# Optimizing a Trainium2 kernel written in Bass

```python
import numpy as np
import jax
import jax.numpy as jnp

def _softmax(x, axis=-1):
    return jax.nn.softmax(x, axis=axis)
def _gelu(x):
    return jax.nn.gelu(x, approximate=True)
def _silu(x):
    return jax.nn.silu(x)
def _sigmoid(x):
    return jax.nn.sigmoid(x)
def _layernorm(x, axis=-1, eps=1e-5):
    m = jnp.mean(x, axis=axis, keepdims=True)
    v = jnp.var(x, axis=axis, keepdims=True)
    return (x - m) / jnp.sqrt(v + eps)
def _scatter_add(tgt, idx, src, axis=0):
    return tgt.at[idx].add(src)
def _segment_sum(src, seg, n):
    return jax.ops.segment_sum(src, seg, n)

kernel_name = 'mk_conv_preact_d2_conv_nchw256_d2b389'

def setup_inputs(seed: int = 0):
    np.random.seed(seed)
    _w = jnp.asarray
    def _rec_inputs():
        import jax
        import jax.numpy as jnp
        _gk = jax.random.key(seed)
        x = -0.0003929 + 0.9999 * jax.random.normal(jax.random.fold_in(_gk, 1), (4, 256, 128, 128), jnp.float32)
        return x
    x = _rec_inputs()
    def _L0_conv_setup():
        import jax, jax.numpy as jnp
        import numpy as np
        HEADS = 4
        WIN = 4
        MAX_N = 5
        DIM = 256

        def _rel_pos_index(N, wh, ww, md, mh, mw):
            cd, ch, cw = (np.arange(N), np.arange(wh), np.arange(ww))
            coords = np.stack(np.meshgrid(cd, ch, cw, indexing='ij')).reshape(3, -1)
            rel = (coords[:, :, None] - coords[:, None, :]).transpose(1, 2, 0).astype(np.int64)
            rel[..., 0] += md - 1
            rel[..., 1] += mh - 1
            rel[..., 2] += mw - 1
            rel[..., 0] *= (2 * mh - 1) * (2 * mw - 1)
            rel[..., 1] *= 2 * mw - 1
            return jnp.asarray(rel.sum(-1))
        key = jax.random.key(seed)
        k1, k2, k3, k4 = jax.random.split(key, 4)
        x = jax.random.normal(k1, (4, DIM, 128, 128), jnp.float32)
        w_qkv = jax.random.normal(k2, (DIM, 3 * DIM), jnp.float32) * DIM ** (-0.5)
        w_out = jax.random.normal(k3, (DIM, DIM), jnp.float32) * DIM ** (-0.5)
        n_bias = (2 * MAX_N - 1) * (2 * WIN - 1) * (2 * WIN - 1)
        bias_table = jax.random.normal(k4, (n_bias, HEADS), jnp.float32) * 0.02
        return {'x': x, 'w_qkv': w_qkv, 'w_out': w_out, 'bias_table': bias_table}
    _L0_conv_all = _L0_conv_setup()
    _L0_conv_in = {k: v for k, v in _L0_conv_all.items() if k in ('w_qkv', 'w_out', 'bias_table', )}
    del _L0_conv_all

    def _L1_conv_setup():
        import jax
        import jax.numpy as jnp
        import numpy as np
        EPS = 1e-05
        B, C, H, W = (64, 256, 56, 56)

        def _finch_labels(data):
            b = data.shape[0]
            nrm = data / jnp.linalg.norm(data, axis=1, keepdims=True)
            dist = 1.0 - nrm @ nrm.T
            idx = jnp.arange(b)
            dist = dist.at[idx, idx].set(jnp.inf)
            nn_idx = jnp.argmin(dist, axis=1)
            N = jnp.eye(b, dtype=jnp.float32) + jax.nn.one_hot(nn_idx, b, dtype=jnp.float32)
            A = N @ N.T
            A = A.at[idx, idx].set(0.0)
            adj = A > 0

            def body(_, labels):
                nbr_min = jnp.min(jnp.where(adj, labels[None, :], b), axis=1)
                return jnp.minimum(labels, nbr_min)
            labels = jax.lax.fori_loop(0, b, body, jnp.arange(b, dtype=jnp.int32))
            return labels
        key = jax.random.key(seed)
        k1, k2, k3, k4, k5 = jax.random.split(key, 5)
        return {'x': jax.random.normal(k1, (B, C, H, W), dtype=jnp.float32), 'running_mean': jax.random.normal(k2, (C,), dtype=jnp.float32), 'running_var': jax.random.uniform(k3, (C,), dtype=jnp.float32), 'weight': jax.random.normal(k4, (C,), dtype=jnp.float32), 'bias': jax.random.normal(k5, (C,), dtype=jnp.float32), 'source_rate': jnp.asarray(0.8, dtype=jnp.float32)}
    _L1_conv_all = _L1_conv_setup()
    _L1_conv_in = {k: v for k, v in _L1_conv_all.items() if k in ('running_mean', 'running_var', 'weight', 'bias', 'source_rate', )}
    del _L1_conv_all

    return {
        "x": x,
        "L0_conv_w_qkv": _L0_conv_in["w_qkv"],
        "L0_conv_w_out": _L0_conv_in["w_out"],
        "L0_conv_bias_table": _L0_conv_in["bias_table"],
        "L1_conv_running_mean": _L1_conv_in["running_mean"],
        "L1_conv_running_var": _L1_conv_in["running_var"],
        "L1_conv_weight": _L1_conv_in["weight"],
        "L1_conv_bias": _L1_conv_in["bias"],
        "L1_conv_source_rate": _L1_conv_in["source_rate"],
    }

def reference(x, L0_conv_w_qkv, L0_conv_w_out, L0_conv_bias_table, L1_conv_running_mean, L1_conv_running_var, L1_conv_weight, L1_conv_bias, L1_conv_source_rate):
    import jax
    import jax.numpy as jnp
    def _L0_conv_ref(x, w_qkv, w_out, bias_table):
        import jax, jax.numpy as jnp
        import numpy as np
        HEADS = 4
        WIN = 4
        MAX_N = 5
        DIM = 256

        def _rel_pos_index(N, wh, ww, md, mh, mw):
            cd, ch, cw = (np.arange(N), np.arange(wh), np.arange(ww))
            coords = np.stack(np.meshgrid(cd, ch, cw, indexing='ij')).reshape(3, -1)
            rel = (coords[:, :, None] - coords[:, None, :]).transpose(1, 2, 0).astype(np.int64)
            rel[..., 0] += md - 1
            rel[..., 1] += mh - 1
            rel[..., 2] += mw - 1
            rel[..., 0] *= (2 * mh - 1) * (2 * mw - 1)
            rel[..., 1] *= 2 * mw - 1
            return jnp.asarray(rel.sum(-1))
        n, C, H, W = x.shape
        dh = C // HEADS
        scale = dh ** (-0.5)
        nh, nw = (H // WIN, W // WIN)
        nwin = nh * nw
        T = MAX_N * WIN * WIN
        xp = jnp.pad(x, ((0, MAX_N - n), (0, 0), (0, 0), (0, 0)))
        t = xp.transpose(0, 2, 3, 1).reshape(MAX_N, nh, WIN, nw, WIN, C)
        xw = t.transpose(1, 3, 0, 2, 4, 5).reshape(nwin, T, C)
        qkv = xw @ w_qkv
        q, k, v = jnp.split(qkv, 3, axis=-1)

        def to_heads(a):
            return a.reshape(nwin, T, HEADS, dh).transpose(0, 2, 1, 3)
        q, k, v = (to_heads(q) * scale, to_heads(k), to_heads(v))
        sim = jnp.einsum('bhid,bhjd->bhij', q, k)
        rpi = _rel_pos_index(MAX_N, WIN, WIN, MAX_N, WIN, WIN)
        sim = sim + bias_table[rpi].transpose(2, 0, 1)
        amask = jnp.repeat(jnp.arange(MAX_N) < n, WIN * WIN)
        pair = amask[:, None] & amask[None, :]
        sim = jnp.where(pair, sim, -jnp.finfo(sim.dtype).max)
        attn = jax.nn.softmax(sim, axis=-1)
        o = jnp.einsum('bhij,bhjd->bhid', attn, v)
        o = o.transpose(0, 2, 1, 3).reshape(nwin, T, C) @ w_out
        o = o.reshape(nh, nw, MAX_N, WIN, WIN, C).transpose(2, 0, 3, 1, 4, 5)
        o = o.reshape(MAX_N, H, W, C).transpose(0, 3, 1, 2)
        return o[:n]

    def _L1_conv_ref(x, running_mean, running_var, weight, bias, source_rate):
        import jax
        import jax.numpy as jnp
        import numpy as np
        EPS = 1e-05
        B, C, H, W = (64, 256, 56, 56)

        def _finch_labels(data):
            b = data.shape[0]
            nrm = data / jnp.linalg.norm(data, axis=1, keepdims=True)
            dist = 1.0 - nrm @ nrm.T
            idx = jnp.arange(b)
            dist = dist.at[idx, idx].set(jnp.inf)
            nn_idx = jnp.argmin(dist, axis=1)
            N = jnp.eye(b, dtype=jnp.float32) + jax.nn.one_hot(nn_idx, b, dtype=jnp.float32)
            A = N @ N.T
            A = A.at[idx, idx].set(0.0)
            adj = A > 0

            def body(_, labels):
                nbr_min = jnp.min(jnp.where(adj, labels[None, :], b), axis=1)
                return jnp.minimum(labels, nbr_min)
            labels = jax.lax.fori_loop(0, b, body, jnp.arange(b, dtype=jnp.int32))
            return labels
        b, c, h, w = x.shape
        sr = jnp.clip(source_rate, 0.0, 1.0)
        rate_ = 1.0 - sr
        mu = jnp.mean(x, axis=(2, 3))
        sigma2 = jnp.var(x, axis=(2, 3), ddof=1)
        labels = _finch_labels(jax.lax.stop_gradient(mu))
        onehot = jax.nn.one_hot(labels, b, dtype=jnp.float32)
        denom = jnp.sum(onehot, axis=0) + EPS
        cluster_mus = onehot.T @ mu / denom[:, None]
        weighted_sigma2 = onehot.T @ sigma2 / denom[:, None]
        mu_diff2 = (mu[:, None, :] - cluster_mus[None, :, :]) ** 2
        weighted_mu_diff2 = jnp.einsum('blc,bl->lc', mu_diff2, onehot) / denom[:, None]
        cluster_sigma2s = weighted_sigma2 + weighted_mu_diff2
        mu_g = (onehot @ cluster_mus)[:, :, None, None]
        sig_g = (onehot @ cluster_sigma2s)[:, :, None, None]
        mu_b = running_mean.reshape(1, c, 1, 1)
        sigma2_b = running_var.reshape(1, c, 1, 1)
        x_n = (x - (rate_ * mu_g + sr * mu_b)) * jax.lax.rsqrt(rate_ * sig_g + sr * sigma2_b + EPS)
        return x_n * weight.reshape(c, 1, 1) + bias.reshape(c, 1, 1)

    def _gn(v, G=32, eps=1e-5):
        B_, C_, H_, W_ = v.shape
        g = v.reshape(B_, G, C_ // G, H_, W_)
        m = jnp.mean(g, axis=(2, 3, 4), keepdims=True)
        s = jnp.var(g, axis=(2, 3, 4), keepdims=True)
        return ((g - m) / jnp.sqrt(s + eps)).reshape(v.shape)

    def _ln_c(v, eps=1e-6):
        m = jnp.mean(v, axis=1, keepdims=True)
        s = jnp.var(v, axis=1, keepdims=True)
        return (v - m) / jnp.sqrt(s + eps)

    def _ln_t(v, eps=1e-5):
        m = jnp.mean(v, axis=-1, keepdims=True)
        s = jnp.var(v, axis=-1, keepdims=True)
        return (v - m) / jnp.sqrt(s + eps)

    def _to_tokens(v):
        B_, C_, H_, W_ = v.shape
        return v.reshape(B_, C_, H_ * W_).transpose(0, 2, 1)
    def _from_tokens(t, like):
        B_, C_, H_, W_ = like.shape
        return t.transpose(0, 2, 1).reshape(B_, C_, H_, W_)

    x = x + _L0_conv_ref(_gn(x), L0_conv_w_qkv, L0_conv_w_out, L0_conv_bias_table)
    x = x + _L1_conv_ref(_gn(x), L1_conv_running_mean, L1_conv_running_var, L1_conv_weight, L1_conv_bias, L1_conv_source_rate)
    return x


_drawn_inputs = setup_inputs


def setup_inputs(seed=0):
    import zlib

    import numpy as np

    out = dict(_drawn_inputs(seed))
    spreads = {}
    factors = {'L0_conv_bias_table': 22.192}
    for name, (base, spread) in spreads.items():
        noise = np.random.default_rng([zlib.crc32(name.encode()), seed]).standard_normal(out[name].shape)
        drawn = base * np.exp(spread * noise) if base else spread * noise
        out[name] = jnp.asarray(drawn.astype(out[name].dtype))
    for name, factor in factors.items():
        out[name] = (out[name] * factor).astype(out[name].dtype)
    return out
```

```python
import concourse.bass as bass
from concourse import mybir
from contextlib import ExitStack


def conv_preact_kernel(nc, x, w_qkv, w_out, bias_table, running_mean, running_var, weight, bias,
                       source_rate, out):
    f32, f32r = mybir.dt.float32, mybir.dt.float32r
    ALU, ACT, AX = mybir.AluOpType, mybir.ActivationFunctionType, mybir.AxisListType

    NIMG, CH, H, W = x.shape
    P = 128
    KC = CH // P
    HEADS, WIN, MAXN = 4, 4, 5
    DH = CH // HEADS
    PIX = WIN * WIN
    TOK = NIMG * PIX
    HP = HEADS // 2
    STRIPS = H // WIN
    STEPS_PER_STRIP = 4
    WPS = W // WIN // STEPS_PER_STRIP
    WP = WPS // 2
    NT = WPS * TOK
    NSTEP = STRIPS * STEPS_PER_STRIP
    ROW = WIN * W
    STRIP = KC * NIMG * ROW
    SLOTS = 4
    SLOTS2 = SLOTS + 2
    BK = NIMG * KC
    HW = H * W
    NCHUNK = HW // 512
    GROUP = CH // 32
    GN_EPS, BN_EPS, CL_EPS = 1e-5, 1e-5, 1e-5
    QSCALE = float(DH) ** -0.5
    NREL = 2 * WIN - 1

    x_bk = x.rearrange("b (k p) h w -> (b k) p (h w)", p=P)
    x_strips = [x[:, k * P:(k + 1) * P, :, :].rearrange("b p (s r) w -> s p b (r w)", r=WIN)
                for k in range(KC)]
    out_strips = [out[:, k * P:(k + 1) * P, :, :].rearrange("b p (s r) w -> s p b (r w)", r=WIN)
                  for k in range(KC)]

    x1_dram = nc.dram_tensor("x1_strips", [STRIPS, P, STRIP], f32, kind="Internal").ap()
    rel_c = nc.dram_tensor("rel_c", [(2 * MAXN - 1) * NREL, PIX * HEADS], f32, kind="Internal").ap()
    rel_rc = nc.dram_tensor("rel_rc", [2 * MAXN - 1, PIX, PIX * HEADS], f32, kind="Internal").ap()

    ctx = ExitStack()
    with ctx:
        def sb(name, shape, dt=f32):
            return ctx.enter_context(nc.sbuf_tensor(name, shape, dt))

        def pb(name, shape):
            return ctx.enter_context(nc.psum_tensor(name, shape, f32))

        def sem(name):
            return ctx.enter_context(nc.semaphore(name))

        xs = sb("xs", [P, SLOTS, STRIP])
        xn = sb("xn", [P, 2, STRIP])
        xhi = [sb(f"xhi{i}", [P, KC, NT], f32r) for i in range(2)]
        xlo = [sb(f"xlo{i}", [P, KC, NT], f32r) for i in range(2)]
        q_sb = sb("q_sb", [P, HP, NT])
        kbd = sb("kbd", [P, HP, WPS, 2, TOK])
        v_sb = [sb(f"v{i}", [P, WP, CH]) for i in range(STEPS_PER_STRIP)]
        prob = [sb(f"prob{i}", [P, WP, HEADS, TOK]) for i in range(2)]
        ptbd = sb("ptbd", [P, WP, HP, 2, 2, TOK])
        ot_hi = sb("ot_hi", [P, HP, NT], f32r)
        ot_lo = sb("ot_lo", [P, HP, NT], f32r)
        wf = sb("wf", [P, KC, 3 * CH])
        whi = sb("whi", [P, KC, 3 * CH], f32r)
        wlo = sb("wlo", [P, KC, 3 * CH], f32r)
        wof = sb("wof", [P, KC, CH])
        wohi = sb("wohi", [P, KC, CH], f32r)
        wolo = sb("wolo", [P, KC, CH], f32r)
        bias_kh = sb("bias_kh", [P, TOK, HEADS])
        bias_sb = sb("bias_sb", [P, HEADS, TOK])
        ident = sb("ident", [P, P])
        gmat = sb("gmat", [P, P])
        ones = sb("ones", [P, P])
        stats = sb("stats", [P, BK, NCHUNK, 6])
        mv = sb("mv", [P, BK, 2])
        rmax = sb("rmax", [P, 2, WP * HEADS])
        rsum = sb("rsum", [P, 2, WP * HEADS])
        rinv = sb("rinv", [P, 2, WP * HEADS])
        gsc = sb("gsc", [P, BK])
        gsh = sb("gsh", [P, BK])
        fin_a = sb("fin_a", [P, BK])
        fin_d = sb("fin_d", [P, BK])
        prm = sb("prm", [P, 4, KC])
        rate = sb("rate", [P, 2])
        sc = sb("sc", [P, 40, 16])
        cube = sb("cube", [P, 2, 64])

        ps_a0 = pb("ps_a0", [P, 1024])
        ps_a1 = pb("ps_a1", [P, 1024])
        ps_b = pb("ps_b", [P, 1024])
        ps_c = pb("ps_c", [P, 1024])

        par_loaded = sem("par_loaded")
        relc_done, relrc_done, bias_loaded = sem("relc_done"), sem("relrc_done"), sem("bias_loaded")
        consts_ready, pads_ready = sem("consts_ready"), sem("pads_ready")
        w_hi_ready, w_lo_ready = sem("w_hi_ready"), sem("w_lo_ready")
        pool_chain = sem("pool_chain")
        p0_loaded = [sem(f"p0_loaded{i}") for i in range(SLOTS)]
        p0_stats = sem("p0_stats")
        small = sem("small")
        to_pe, from_pe = sem("to_pe"), sem("from_pe")
        to_act, from_act = sem("to_act"), sem("from_act")
        x_loaded = sem("x_loaded")
        xn_ready, xhi_ready, xlo_ready = sem("xn_ready"), sem("xhi_ready"), sem("xlo_ready")
        q_done, k_done, v_done = sem("q_done"), sem("k_done"), sem("v_done")
        s_done, t_done, pv_done, out_done = sem("s_done"), sem("t_done"), sem("pv_done"), sem("out_done")
        q_evac, k_evac, v_evac = sem("q_evac"), sem("k_evac"), sem("v_evac")
        biased, max_ready, shifted, exp_done = sem("biased"), sem("max_ready"), sem("shifted"), sem("exp_done")
        sum_ready, inv_ready, norm_done = sem("sum_ready"), sem("inv_ready"), sem("norm_done")
        pt_evac, o_evac, olo_ready, res_done = sem("pt_evac"), sem("o_evac"), sem("olo_ready"), sem("res_done")
        x1_stats, x1_stored = sem("x1_stats"), sem("x1_stored")
        p2_loaded = [sem(f"p2_loaded{i}") for i in range(SLOTS2)]
        p2_stored = [sem(f"p2_stored{i}") for i in range(SLOTS2)]
        fin_done = sem("fin_done")

        def steps(eng, body):
            def strip(i, first, last):
                for g in range(STEPS_PER_STRIP):
                    body(i, g, lambda lag, g=g: (not first or g >= lag) and (not last or g - lag < STEPS_PER_STRIP))
            strip(0, True, False)
            with eng.Fori(1, STRIPS - 1) as i:
                strip(i, False, False)
            strip(STRIPS - 1, False, True)
            for g in range(3):
                body(STRIPS, g, lambda lag, g=g: lag > g)

        def slot(eng, i, n):
            return i % n if isinstance(i, int) else eng.snap(i & (n - 1))

        def xs_at(s, k, lo, n):
            v = xs[:, s:s + 1, :] if isinstance(s, int) else xs[:, bass.ds(s, 1), :]
            v = v.rearrange("p a f -> p (a f)")
            return v[:, k * NIMG * ROW + lo:k * NIMG * ROW + lo + n]

        def xn_at(s):
            v = xn[:, s:s + 1, :] if isinstance(s, int) else xn[:, bass.ds(s, 1), :]
            return v.rearrange("p a f -> p (a f)").rearrange("p (k f) -> p k f", k=KC)

        p2_bufs = [xs[:, s, :] for s in range(SLOTS)] + [xn[:, s, :] for s in range(2)]
        P2_FIRST = [STRIPS - SLOTS + s for s in range(SLOTS)] + [0, 1]
        P2_FULL, P2_REST = divmod(STRIPS - SLOTS2, SLOTS2)

        def p2_strip(r, s):
            return r * SLOTS2 + (s + 2 - SLOTS2)

        block = ctx.enter_context(nc.Block())

        @block.sync
        def _(sp):
            def piece(t, q):
                return x_bk[t:t + 1, :, q * STRIP:(q + 1) * STRIP] if isinstance(t, int) else \
                    x_bk[bass.ds(t, 1), :, q * STRIP:(q + 1) * STRIP]
            for q in range(SLOTS):
                sp.dma_start(xs[:, q, :], piece(0, q).rearrange("a p f -> p (a f)")).then_inc(p0_loaded[q], 16)
            with sp.Fori(1, BK) as t:
                read = [sp.snap(t * SLOTS + (q + 1 - SLOTS)) for q in range(SLOTS)]
                for q in range(SLOTS):
                    sp.wait_ge(p0_stats, read[q])
                    sp.dma_start(xs[:, q, :], piece(t, q).rearrange("a p f -> p (a f)")).then_inc(p0_loaded[q], 16)

            def load(i, s):
                for k in range(KC):
                    src = x_strips[k][i:i + 1] if isinstance(i, int) else x_strips[k][bass.ds(i, 1)]
                    v = xs[:, s:s + 1, :] if isinstance(s, int) else xs[:, bass.ds(s, 1), :]
                    v = v.rearrange("p a f -> p (a f)")[:, k * NIMG * ROW:(k + 1) * NIMG * ROW]
                    sp.dma_start(v.rearrange("p (b f) -> p b f", b=NIMG),
                                 src.rearrange("a p b f -> p (a b) f")).then_inc(x_loaded, 16)

            for i in range(SLOTS - 1):
                sp.wait_ge(p0_stats, (BK - 1) * SLOTS + i + 1)
                if i:
                    sp.wait_ge(x_loaded, 32 * i)
                load(i, i)
            sp.wait_ge(p0_stats, BK * SLOTS)
            sp.wait_ge(x_loaded, 32 * (SLOTS - 1))
            load(SLOTS - 1, SLOTS - 1)

            def store(m, s):
                dst = x1_dram[m:m + 1] if isinstance(m, int) else x1_dram[bass.ds(m, 1)]
                v = xs[:, s:s + 1, :] if isinstance(s, int) else xs[:, bass.ds(s, 1), :]
                sp.dma_start(dst.rearrange("a p f -> p (a f)"), v.rearrange("p a f -> p (a f)")).then_inc(x1_stored, 16)

            with sp.Fori(1, STRIPS - SLOTS + 1) as i:
                s = slot(sp, i + (SLOTS - 1), SLOTS)
                before, ahead = sp.snap(i - 1), sp.snap(i + (SLOTS - 1))
                steps_before, stored, loaded = sp.snap(i * STEPS_PER_STRIP), sp.snap(i * 16), sp.snap(i * 32 + 32 * (SLOTS - 1))
                sp.wait_ge(res_done, steps_before)
                store(before, s)
                sp.wait_ge(x1_stats, stored)
                sp.wait_ge(x1_stored, stored)
                sp.wait_ge(x_loaded, loaded)
                load(ahead, s)

            sp.wait_ge(xlo_ready, NSTEP)
            sp.wait_ge(xhi_ready, NSTEP)
            sp.wait_ge(x1_stored, 16 * (STRIPS - SLOTS))
            for s in range(SLOTS, SLOTS2):
                sp.dma_start(p2_bufs[s], x1_dram[P2_FIRST[s], :, :]).then_inc(p2_loaded[s], 16)
            with sp.Fori(1, P2_FULL + 1) as r:
                strips = [sp.snap(p2_strip(r, s)) for s in range(SLOTS2)]
                written = sp.snap(r * 32)
                for s in range(SLOTS2):
                    sp.wait_ge(p2_stored[s], written)
                    sp.dma_start(p2_bufs[s], x1_dram[bass.ds(strips[s], 1)].rearrange("a p f -> p (a f)"))\
                        .then_inc(p2_loaded[s], 16)
            for s in range(P2_REST):
                sp.wait_ge(p2_stored[s], 32 * (P2_FULL + 1))
                sp.dma_start(p2_bufs[s], x1_dram[p2_strip(P2_FULL + 1, s), :, :]).then_inc(p2_loaded[s], 16)

        @block.gpsimd
        def _(pool):
            pool.memset(ident[:], 0.0).then_inc(pool_chain, 1)
            pool.memset(gmat[:], 1.0 / GROUP).then_inc(pool_chain, 1)
            pool.memset(ones[:], 1.0).then_inc(consts_ready, 1)
            pool.wait_ge(pool_chain, 2)
            pool.affine_select(out=ident[:], in_=ident[:], compare_op=ALU.not_equal, fill=1.0, base=0,
                               pattern=[[-1, P]], channel_multiplier=1).then_inc(consts_ready, 1)
            g3 = gmat[:].rearrange("p (g j) -> p g j", j=GROUP)
            pool.affine_select(out=g3, in_=g3, compare_op=ALU.is_ge, fill=0.0, base=0,
                               pattern=[[-GROUP, P // GROUP], [0, GROUP]], channel_multiplier=1).then_inc(pool_chain, 1)
            pool.wait_ge(pool_chain, 3)
            pool.affine_select(out=g3, in_=g3, compare_op=ALU.is_ge, fill=0.0, base=GROUP - 1,
                               pattern=[[GROUP, P // GROUP], [0, GROUP]], channel_multiplier=-1).then_inc(consts_ready, 1)
            pool.memset(kbd[:], 0.0).then_inc(pads_ready, 1)
            pool.memset(ptbd[:], 0.0).then_inc(pads_ready, 1)
            for n, (lo, full, hi) in enumerate(((wlo, wf, whi), (wolo, wof, wohi))):
                pool.wait_ge(w_hi_ready, n + 1)
                pool.tensor_tensor(lo[:], full[:], hi[:], ALU.subtract).then_inc(w_lo_ready, 1)

            def low_part(i, g, m):
                src = xn_at(slot(pool, i, 2))[:, :, g * NT:(g + 1) * NT]
                pool.wait_ge(xhi_ready, m + 1)
                pool.tensor_tensor(xlo[g % 2][:], src, xhi[g % 2][:], ALU.subtract).then_inc(xlo_ready, 1)

            low_part(0, 0, 0)

            def body(i, g, ok):
                n = i * STEPS_PER_STRIP + g
                if ok(1):
                    pool.wait_ge(max_ready, n)
                    j = (g - 1) % 2
                    p3 = prob[j][:].rearrange("p w h t -> p (w h) t")
                    pool.tensor_tensor(p3, p3, rmax[:, j, :].unsqueeze(2).broadcast_to([P, WP * HEADS, TOK]),
                                       ALU.subtract).then_inc(shifted, 1)
                if ok(-1):
                    pool_i, pool_g = (i, g + 1) if g + 1 < STEPS_PER_STRIP else (i + 1, 0)
                    low_part(pool_i, pool_g, n + 1)
                if ok(1):
                    pool.wait_ge(inv_ready, n)
                    pool.tensor_tensor(p3, p3, rinv[:, j, :].unsqueeze(2).broadcast_to([P, WP * HEADS, TOK]),
                                       ALU.mult).then_inc(norm_done, 1)

            steps(pool, body)

        @block.scalar
        def _(act):
            act.dma_start(wf[:], w_qkv.rearrange("(k p) n -> p k n", p=P)).then_inc(par_loaded, 16)
            act.dma_start(wof[:], w_out.rearrange("(k p) n -> p k n", p=P)).then_inc(par_loaded, 16)
            for n, v in enumerate((running_mean, running_var, weight, bias)):
                for k in range(KC):
                    act.dma_start(prm[:, n, k:k + 1], v[k * P:(k + 1) * P].unsqueeze(1)).then_inc(par_loaded, 16)
            act.dma_start(rate[:, 0:1], source_rate.broadcast_to([P, 1])).then_inc(par_loaded, 16)

            TE, F = HEADS, PIX * HEADS
            for c1 in range(WIN):
                src = bass.AP(bias_table.tensor, (c1 + WIN - 1) * TE,
                              [[NREL * TE, (2 * MAXN - 1) * NREL], [-TE, WIN], [1, TE]])
                act.dma_start(rel_c[:, c1 * WIN * TE:(c1 + 1) * WIN * TE].rearrange("a (c h) -> a c h", h=TE), src)\
                    .then_inc(relc_done, 16)
            act.wait_ge(relc_done, 16 * WIN)
            for r1 in range(WIN):
                for c1 in range(WIN):
                    src = bass.AP(rel_c.tensor, (r1 + WIN - 1) * F + c1 * WIN * TE,
                                  [[NREL * F, 2 * MAXN - 1], [-F, WIN], [1, WIN * TE]])
                    act.dma_start(rel_rc[:, r1 * WIN + c1, :].rearrange("a (r e) -> a r e", r=WIN), src)\
                        .then_inc(relrc_done, 16)
            act.wait_ge(relrc_done, 16 * PIX)
            for half in range(2):
                for f1 in range(NIMG):
                    src = bass.AP(rel_rc.tensor, (f1 + MAXN - 1) * PIX * F, [[F, PIX], [-PIX * F, NIMG], [1, F]])
                    q0 = half * TOK + f1 * PIX
                    act.dma_start(bias_kh[q0:q0 + PIX].rearrange("p (f t) h -> p f (t h)", f=NIMG), src)\
                        .then_inc(bias_loaded, 16)

            act.wait_ge(par_loaded, 16 * (3 + 4 * KC))
            act.activation(whi[:], wf[:], ACT.Copy).then_inc(w_hi_ready, 1)
            act.activation(wohi[:], wof[:], ACT.Copy).then_inc(w_hi_ready, 1)

            act.wait_ge(to_act, 1)
            act.activation(sc[:, 1, 0:BK], sc[:, 0, 0:BK], ACT.Sqrt).then_inc(from_act, 1)

            def normalise(i, piece):
                k, b = divmod(piece, NIMG)
                src = xs_at(slot(act, i, SLOTS), k, b * ROW, ROW).rearrange("p (r w c) -> p w r c", r=WIN, c=WIN)
                dst = xn_at(slot(act, i, 2))[:, k, :].rearrange("p (w b r c) -> p b w r c", b=NIMG, r=WIN, c=WIN)[:, b]
                j = b * KC + k
                act.activation(dst, src, ACT.Identity, bias=gsh[:, j:j + 1], scale=gsc[:, j:j + 1]).then_inc(xn_ready, 1)

            act.wait_ge(small, SMALL_GN0)
            act.wait_ge(x_loaded, 32)
            for piece in range(BK):
                normalise(0, piece)
            act.wait_ge(pads_ready, 2)

            def body(i, g, ok):
                n = i * STEPS_PER_STRIP + g
                if ok(-STEPS_PER_STRIP):
                    if g == 0:
                        act.wait_ge(x_loaded, i * 32 + 64)
                        if not isinstance(i, int) or i > 0:
                            act.wait_ge(xhi_ready, i * STEPS_PER_STRIP)
                            act.wait_ge(xlo_ready, i * STEPS_PER_STRIP)
                    nxt = i + 1 if isinstance(i, int) else act.snap(i + 1)
                    normalise(nxt, 2 * g)
                    normalise(nxt, 2 * g + 1)
                if ok(0):
                    act.wait_ge(q_done, n + 1)
                    act.activation(q_sb[:].rearrange("p a t -> p (a t)"), ps_a0[:], ACT.Copy, scale=QSCALE).then_inc(q_evac, 1)
                    act.wait_ge(k_done, n + 1)
                    for hh in range(2):
                        rows = slice(hh * DH, (hh + 1) * DH)
                        ins = act.activation(kbd[rows, :, :, hh, :].rearrange("p a w t -> p (a w) t"),
                                             ps_a1[rows, :].rearrange("p (aw t) -> p aw t", t=TOK), ACT.Copy)
                    ins.then_inc(k_evac, 1)
                if ok(2):
                    act.wait_ge(t_done, n - 1)
                    for hh in range(2):
                        for ww in range(2):
                            ins = act.activation(
                                ptbd[ww * TOK:(ww + 1) * TOK, :, :, hh, ww, :].rearrange("p w a t -> p (w a) t"),
                                ps_c[hh * TOK:(hh + 1) * TOK, :].rearrange("p (wa v t) -> p wa v t", v=2, t=TOK)[:, :, ww, :],
                                ACT.Copy)
                    ins.then_inc(pt_evac, 1)
                if ok(1):
                    act.wait_ge(shifted, n)
                    p2 = prob[(g - 1) % 2][:].rearrange("p w h t -> p (w h t)")
                    act.activation(p2, p2, ACT.Exp).then_inc(exp_done, 1)
                if ok(0):
                    act.wait_ge(v_done, n + 1)
                    act.activation(v_sb[g][:].rearrange("p w c -> p (w c)"), ps_a0[:], ACT.Copy).then_inc(v_evac, 1)
                if ok(2):
                    act.wait_ge(pv_done, n - 1)
                    act.activation(ot_hi[:].rearrange("p a t -> p (a t)"), ps_c[:], ACT.Copy).then_inc(o_evac, 1)

            steps(act, body)

            for r in range(2):
                act.wait_ge(to_act, 2 + r)
                act.activation(sc[:, 1, 0:BK], sc[:, 0, 0:BK], ACT.Sqrt).then_inc(from_act, 1)
            act.wait_ge(to_act, 4)
            act.activation(sc[:, 1, 0:BK], sc[:, 0, 0:BK], ACT.Sqrt).then_inc(from_act, 1)

            def store(m, s, count):
                act.wait_ge(fin_done, count)
                for k in range(KC):
                    dst = out_strips[k][m:m + 1] if isinstance(m, int) else out_strips[k][bass.ds(m, 1)]
                    act.dma_start(dst.rearrange("a p b f -> p (a b) f"),
                                  p2_bufs[s][:, k * NIMG * ROW:(k + 1) * NIMG * ROW].rearrange("p (b f) -> p b f", b=NIMG))\
                        .then_inc(p2_stored[s], 16)
            for s in range(SLOTS2):
                store(P2_FIRST[s], s, s + 1)
            with act.Fori(1, P2_FULL + 1) as r:
                for s in range(SLOTS2):
                    store(act.snap(p2_strip(r, s)), s, r * SLOTS2 + (s + 1))
            for s in range(P2_REST):
                store(p2_strip(P2_FULL + 1, s), s, (P2_FULL + 1) * SLOTS2 + s + 1)
            for s in range(SLOTS2):
                act.wait_ge(p2_stored[s], 32 * (P2_FULL + 1 + (s < P2_REST)))

        @block.tensor
        def _(pe):
            def small_mm(n, dst, lhsT, parts):
                pe.wait_ge(to_pe, n)
                for j, r in enumerate(parts):
                    ins = pe.matmul(dst, lhsT, r, start=(j == 0), stop=(j == len(parts) - 1))
                ins.then_inc(from_pe, 1)

            pe.wait_ge(consts_ready, 3)
            pe.wait_ge(w_lo_ready, 2)
            small_mm(1, ps_b[:, 0:BK], gmat[:], [sc[:, 2, 0:BK]])
            small_mm(2, ps_b[:, 0:BK], gmat[:], [sc[:, 3, 0:BK]])

            def body(i, g, ok):
                n = i * STEPS_PER_STRIP + g
                hi, lo = xhi[g % 2], xlo[g % 2]

                def project_qk(ps, col0):
                    for a in range(HP):
                        cols = slice(col0 + a * P, col0 + (a + 1) * P)
                        terms = [(w[:, k, cols], t[:, k, :]) for k in range(KC) for w, t in ((whi, hi), (whi, lo), (wlo, hi))]
                        for j, (w, t) in enumerate(terms):
                            ins = pe.matmul(ps[:, a * NT:(a + 1) * NT], w, t, start=(j == 0), stop=(j == len(terms) - 1))
                    return ins

                if ok(1):
                    pe.wait_ge(q_evac, n)
                    pe.wait_ge(k_evac, n)
                    if ok(4):
                        pe.wait_ge(res_done, n - 3)
                    elif ok(2):
                        pe.wait_ge(biased, n - 1)
                    for w in range(WPS):
                        rows = slice(w % 2 * TOK, (w % 2 + 1) * TOK)
                        for a in range(HP):
                            c = w // 2 * HEADS * TOK + a * 2 * TOK
                            ins = pe.matmul(ps_b[rows, c:c + 2 * TOK], q_sb[:, a, w * TOK:(w + 1) * TOK],
                                            kbd[:, a, w, :, :].rearrange("p h t -> p (h t)"), start=True, stop=True)
                    ins.then_inc(s_done, 1)
                if ok(0):
                    pe.wait_ge(xhi_ready, n + 1)
                    pe.wait_ge(xlo_ready, n + 1)
                    if ok(1):
                        pe.wait_ge(v_evac, n)
                    project_qk(ps_a0, 0).then_inc(q_done, 1)
                    if ok(1):
                        pe.wait_ge(k_evac, n)
                    project_qk(ps_a1, CH).then_inc(k_done, 1)
                if ok(2):
                    pe.wait_ge(norm_done, n - 1)
                    if ok(3):
                        pe.wait_ge(olo_ready, n - 2)
                    pr = prob[g % 2]
                    for w in range(WP):
                        for a in range(HP):
                            c = (w * HP + a) * P
                            ins = pe.transpose(ps_c[:, c:c + P], pr[:, w, 2 * a:2 * a + 2, :].rearrange("p h t -> p (h t)"), ident[:])
                    ins.then_inc(t_done, 1)
                if ok(0):
                    pe.wait_ge(q_evac, n + 1)
                    for w in range(WP):
                        toks = slice(w * 2 * TOK, (w + 1) * 2 * TOK)
                        terms = [(t[:, k, toks], wt[:, k, 2 * CH:3 * CH]) for k in range(KC) for t, wt in ((hi, whi), (hi, wlo), (lo, whi))]
                        for j, (t, wt) in enumerate(terms):
                            ins = pe.matmul(ps_a0[:, w * CH:(w + 1) * CH], t, wt, start=(j == 0), stop=(j == len(terms) - 1))
                    ins.then_inc(v_done, 1)
                if ok(3):
                    pe.wait_ge(olo_ready, n - 2)
                    if ok(1):
                        pe.wait_ge(biased, n)
                    else:
                        pe.wait_ge(res_done, n - 3)
                    for m in range(KC):
                        terms = [(w[:, k, m * P:(m + 1) * P], t[:, k, :]) for k in range(KC)
                                 for w, t in ((wohi, ot_hi), (wohi, ot_lo), (wolo, ot_hi))]
                        for j, (w, t) in enumerate(terms):
                            ins = pe.matmul(ps_b[:, m * NT:(m + 1) * NT], w, t, start=(j == 0), stop=(j == len(terms) - 1))
                    ins.then_inc(out_done, 1)
                if ok(2):
                    pe.wait_ge(pt_evac, n - 1)
                    pe.wait_ge(v_evac, n - 1)
                    for w in range(WP):
                        for a in range(HP):
                            for hh in range(2):
                                h = 2 * a + hh
                                ins = pe.matmul(ps_c[hh * DH:(hh + 1) * DH, a * NT + w * P:a * NT + (w + 1) * P],
                                                v_sb[(g - 2) % 4][:, w, h * DH:(h + 1) * DH],
                                                ptbd[:, w, a, hh, :, :].rearrange("p v t -> p (v t)"), start=True, stop=True)
                    ins.then_inc(pv_done, 1)

            steps(pe, body)
            small_mm(3, ps_b[:, 0:BK], gmat[:], [sc[:, 2, 0:BK]])
            small_mm(4, ps_b[:, 0:BK], gmat[:], [sc[:, 3, 0:BK]])
            small_mm(5, ps_b[:, 0:16], ones[:], [sc[:, 10, 0:16], sc[:, 11, 0:16]])

        @block.vector
        def _(dve):
            chain = [0]

            def link(ins):
                chain[0] += 1
                ins.then_inc(small, 1)
                dve.wait_ge(small, chain[0])

            asks = {"pe": 0, "act": 0}

            def ask(who):
                asks[who] += 1
                there, back = (to_pe, from_pe) if who == "pe" else (to_act, from_act)
                dve.sem_inc(there, 1)
                dve.wait_ge(back, asks[who])

            TT, TS, STT = dve.tensor_tensor, dve.tensor_scalar, dve.scalar_tensor_tensor

            def rsqrt(dst, v, n):
                ask("act")
                y, t = sc[:, 1, 0:n], sc[:, 4, 0:n]
                link(dve.reciprocal(y, sc[:, 1, 0:n]))
                link(TT(t, y, y, ALU.mult))
                link(TT(t, t, v, ALU.mult))
                link(TS(t, t, -0.5, 1.5, ALU.mult, ALU.add))
                link(TT(dst, y, t, ALU.mult))

            def group_norm():
                for j in range(BK):
                    link(dve.bn_aggr(mv[:, j, :], stats[:, j, :, :].rearrange("p n s -> p (n s)")))
                mean, var = mv[:, :, 0], mv[:, :, 1]
                link(dve.tensor_copy(sc[:, 2, 0:BK], mean))
                ask("pe")
                gm, t = sc[:, 5, 0:BK], sc[:, 6, 0:BK]
                link(dve.tensor_copy(gm, ps_b[:, 0:BK]))
                link(TT(t, sc[:, 2, 0:BK], gm, ALU.subtract))
                link(TT(t, t, t, ALU.mult))
                link(TT(sc[:, 3, 0:BK], t, var, ALU.add))
                ask("pe")
                link(TS(sc[:, 0, 0:BK], ps_b[:, 0:BK], GN_EPS, None, ALU.add))
                rsqrt(gsc[:], sc[:, 0, 0:BK], BK)
                link(STT(out=gsh[:], in0=gm, scalar=-1.0, in1=gsc[:], op0=ALU.mult, op1=ALU.mult))

            def piece_stats(t, q):
                for j in range(STRIP // 512):
                    c = q * (STRIP // 512) + j
                    dst = stats[:, t:t + 1, c, :] if isinstance(t, int) else stats[:, bass.ds(t, 1), c, :]
                    ins = dve.bn_stats(dst.rearrange("p a s -> p (a s)"), xs[:, q, j * 512:(j + 1) * 512])
                ins.then_inc(p0_stats, 1)
            with dve.Fori(0, BK) as t:
                for q in range(SLOTS):
                    dve.wait_ge(p0_loaded[q], t * 16 + 16)
                    piece_stats(t, q)
            dve.wait_ge(p0_stats, BK * SLOTS)
            group_norm()
            assert chain[0] == SMALL_GN0, chain[0]
            dve.wait_ge(bias_loaded, 16 * 8)
            link(dve.tensor_copy(bias_sb[:], bias_kh[:].rearrange("p t h -> p h t")))

            def t(n, w=BK):
                return sc[:, n, 0:w]

            def kb(ap):
                return ap.rearrange("p (b k) -> p k b", k=KC)

            def sq(ap):
                return ap.rearrange("p (i j) -> p i j", j=NIMG)

            def over_i(ap):
                return ap.unsqueeze(2).broadcast_to([P, NIMG, NIMG])

            def over_j(ap):
                return ap.unsqueeze(1).broadcast_to([P, NIMG, NIMG])

            idx, eye, mixed = t(14, NIMG), t(15, 16), t(35, 4)
            for b in range(NIMG):
                link(dve.memset(sc[:, 14, b:b + 1], float(b - NIMG)))
            link(TT(sq(eye), over_i(idx), over_j(idx), ALU.is_equal))
            dve.wait_ge(par_loaded, 16 * (3 + 4 * KC))
            link(TS(rate[:, 0:1], rate[:, 0:1], 0.0, 1.0, ALU.max, ALU.min))
            link(TS(rate[:, 1:2], rate[:, 0:1], -1.0, 1.0, ALU.mult, ALU.add))
            link(TS(mixed, prm[:, 0:2, :].rearrange("p a k -> p (a k)"), rate[:, 0:1], None, ALU.mult))

            def high_part(i, g):
                src = xn_at(slot(dve, i, 2))[:, :, g * NT:(g + 1) * NT]
                dve.tensor_copy(xhi[g % 2][:], src).then_inc(xhi_ready, 1)

            dve.wait_ge(xn_ready, BK)
            high_part(0, 0)

            def body(i, g, ok):
                n = i * STEPS_PER_STRIP + g
                j = (g - 1) % 2
                p3 = prob[j][:].rearrange("p w h t -> p (w h) t")
                if ok(3):
                    dve.wait_ge(o_evac, n - 2)
                    TT(ot_lo[:].rearrange("p a t -> p (a t)"), ps_c[:], ot_hi[:].rearrange("p a t -> p (a t)"),
                       ALU.subtract).then_inc(olo_ready, 1)
                if ok(1):
                    dve.wait_ge(s_done, n)
                    TT(prob[j][:].rearrange("p w h t -> p w (h t)"), ps_b[:].rearrange("p (w f) -> p w f", w=WP),
                       bias_sb[:].rearrange("p h t -> p (h t)").unsqueeze(1).broadcast_to([P, WP, HEADS * TOK]),
                       ALU.add).then_inc(biased, 1)
                    dve.wait_ge(biased, n)
                    dve.tensor_reduce(rmax[:, j, :], p3, AX.X, ALU.max).then_inc(max_ready, 1)
                if ok(-1):
                    ni, ng = (i, g + 1) if g + 1 < STEPS_PER_STRIP else (i + 1, 0)
                    if ng == 0:
                        dve.wait_ge(xn_ready, i * BK + 2 * BK)
                        ni = ni if isinstance(ni, int) else dve.snap(ni)
                    if ok(1):
                        dve.wait_ge(v_done, n)
                    high_part(ni, ng)
                if ok(1):
                    dve.wait_ge(exp_done, n)
                    dve.tensor_reduce(rsum[:, j, :], p3, AX.X, ALU.add).then_inc(sum_ready, 1)
                    dve.wait_ge(sum_ready, n)
                    dve.reciprocal(rinv[:, j, :], rsum[:, j, :]).then_inc(inv_ready, 1)
                if ok(3):
                    dve.wait_ge(out_done, n - 2)
                    sg = (g - 3) % 4
                    si = i if g == 3 else (i - 1 if isinstance(i, int) else dve.snap(i - 1))
                    s = slot(dve, si, SLOTS)
                    for m in range(KC):
                        v = xs_at(s, m, 0, NIMG * ROW).rearrange("p (br w) -> p br w", w=W)
                        v = v[:, :, sg * WPS * WIN:(sg + 1) * WPS * WIN].rearrange("p br (j c) -> p br j c", c=WIN)
                        o = ps_b[:, m * NT:(m + 1) * NT].rearrange("p (j br c) -> p br j c", br=NIMG * WIN, c=WIN)
                        ins = TT(v, o, v, ALU.add)
                    ins.then_inc(res_done, 1)
                strip_done = (g == 3 and (not isinstance(i, int) or 0 < i < STRIPS)) or (isinstance(i, int) and i == STRIPS and g == 2)
                if strip_done:
                    dve.wait_ge(res_done, i * STEPS_PER_STRIP)
                    si = i - 1 if isinstance(i, int) else dve.snap(i - 1)
                    s = slot(dve, si, SLOTS)
                    for k in range(KC):
                        for b in range(NIMG):
                            dst = stats[:, b * KC + k, si:si + 1, :] if isinstance(si, int) else stats[:, b * KC + k, bass.ds(si, 1), :]
                            ins = dve.bn_stats(dst.rearrange("p a s -> p (a s)"), xs_at(s, k, b * ROW, ROW))
                    ins.then_inc(x1_stats, 16)

            steps(dve, body)

            dve.wait_ge(x1_stats, 16 * STRIPS)
            group_norm()

            mu, sg2 = t(7), t(8)
            link(TT(mu, mv[:, :, 0], sc[:, 5, 0:BK], ALU.subtract))
            link(TT(mu, mu, gsc[:], ALU.mult))
            link(TT(sg2, mv[:, :, 1], gsc[:], ALU.mult))
            link(TT(sg2, sg2, gsc[:], ALU.mult))
            link(TS(sg2, sg2, float(HW) / (HW - 1), None, ALU.mult))
            for k in range(KC):
                m_k = kb(mu)[:, k, :]
                link(TT(t(10 + k, 16).rearrange("p (i j) -> p i j", j=NIMG), m_k.unsqueeze(2).broadcast_to([P, NIMG, NIMG]),
                        m_k.unsqueeze(1).broadcast_to([P, NIMG, NIMG]), ALU.mult))
            ask("pe")
            gram = t(12, 16)
            link(dve.tensor_copy(gram, ps_b[:, 0:16]))
            link(dve.memset(sc[:, 0, 0:BK], 1.0))
            link(dve.tensor_copy(sc[:, 0, 0:NIMG], gram[:, 0:16:NIMG + 1]))
            rn = t(13, BK)
            rsqrt(rn, sc[:, 0, 0:BK], BK)

            dist = t(16, 16)
            link(TT(sq(dist), sq(gram), over_i(rn[:, 0:NIMG]), ALU.mult))
            link(TT(sq(dist), sq(dist), over_j(rn[:, 0:NIMG]), ALU.mult))
            link(TS(dist, dist, -1.0, 1.0, ALU.mult, ALU.add))
            link(STT(out=dist, in0=eye, scalar=1e30, in1=dist, op0=ALU.mult, op1=ALU.add))
            dmin, cand, nn = t(17, NIMG), t(18, 16), t(19, NIMG)
            link(dve.tensor_reduce(dmin, sq(dist), AX.X, ALU.min))
            link(TT(sq(cand), sq(dist), over_i(dmin), ALU.is_equal))

            def masked_min(dst, mask, values):
                link(TT(sq(t(21, 16)), sq(mask), over_j(values), ALU.mult))
                link(dve.tensor_reduce(dst, sq(t(21, 16)), AX.X, ALU.min))

            masked_min(nn, cand, idx)
            nbr, adj = t(22, 16), t(23, 16)
            link(TT(sq(nbr), over_i(nn), over_j(idx), ALU.is_equal))
            link(TT(nbr, nbr, eye, ALU.add))
            c3 = cube[:, 0, :].rearrange("p (i j m) -> p i j m", j=NIMG, m=NIMG)
            link(TT(c3, sq(nbr).unsqueeze(2).broadcast_to([P, NIMG, NIMG, NIMG]),
                    sq(nbr).unsqueeze(1).broadcast_to([P, NIMG, NIMG, NIMG]), ALU.mult))
            link(dve.tensor_reduce(sq(adj), c3, AX.X, ALU.add))
            link(TS(adj, adj, 0.0, None, ALU.is_gt))
            link(STT(out=t(24, 16), in0=eye, scalar=-1.0, in1=adj, op0=ALU.mult, op1=ALU.add))
            link(TS(adj, t(24, 16), 0.0, None, ALU.is_gt))
            lab, near = t(25, NIMG), t(26, NIMG)
            link(dve.tensor_copy(lab, idx))
            for _ in range(NIMG - 1):
                masked_min(near, adj, lab)
                link(TT(lab, lab, near, ALU.min))
            oh, ohT, den = t(27, 16), t(28, 16), t(29, NIMG)
            link(TT(sq(oh), over_i(lab), over_j(idx), ALU.is_equal))
            link(dve.tensor_copy(sq(ohT), oh.rearrange("p (i l) -> p l i", l=NIMG)))
            link(dve.tensor_reduce(den, sq(ohT), AX.X, ALU.add))
            link(TS(den, den, CL_EPS, None, ALU.add))
            rden = t(39, NIMG)
            link(dve.reciprocal(rden, den))

            KLI = [P, KC, NIMG, NIMG]
            c4 = [cube[:, c, 0:32].rearrange("p (k l i) -> p k l i", k=KC, l=NIMG) for c in range(2)]

            def k3(ap):
                return ap.rearrange("p (k l) -> p k l", k=KC)

            def weighted(dst, vals):
                link(TT(c4[1], sq(ohT).unsqueeze(1).broadcast_to(KLI), vals, ALU.mult))
                link(dve.tensor_reduce(k3(dst), c4[1], AX.X, ALU.add))
                link(TT(k3(dst), k3(dst), rden.unsqueeze(1).broadcast_to([P, KC, NIMG]), ALU.mult))

            cm, cs, cd = t(30), t(31), t(32)
            weighted(cm, kb(mu).unsqueeze(2).broadcast_to(KLI))
            weighted(cs, kb(sg2).unsqueeze(2).broadcast_to(KLI))
            link(TT(c4[0], kb(mu).unsqueeze(2).broadcast_to(KLI), k3(cm).unsqueeze(3).broadcast_to(KLI), ALU.subtract))
            link(TT(c4[0], c4[0], c4[0], ALU.mult))
            weighted(cd, c4[0])
            link(TT(cs, cs, cd, ALU.add))

            def of_image(dst, per_cluster):
                link(TT(c4[1], sq(oh).unsqueeze(1).broadcast_to(KLI), k3(per_cluster).unsqueeze(2).broadcast_to(KLI), ALU.mult))
                link(dve.tensor_reduce(k3(dst), c4[1], AX.X, ALU.add))

            mug, sgg = t(33), t(34)
            of_image(mug, cm)
            of_image(sgg, cs)
            for n, v in enumerate((mug, sgg)):
                link(STT(out=k3(v), in0=k3(v), scalar=rate[:, 1:2], in1=mixed[:, n * KC:(n + 1) * KC].unsqueeze(2).broadcast_to([P, KC, NIMG]),
                         op0=ALU.mult, op1=ALU.add))
            link(TS(sc[:, 0, 0:BK], sgg, BN_EPS, None, ALU.add))
            rw = t(36)
            rsqrt(rw, sc[:, 0, 0:BK], BK)
            link(TT(k3(rw), k3(rw), prm[:, 2, :].unsqueeze(2).broadcast_to([P, KC, NIMG]), ALU.mult))
            link(TT(k3(t(37)), k3(rw), kb(gsc[:]), ALU.mult))
            link(TS(fin_a[:], t(37), 1.0, None, ALU.add))
            link(TT(k3(t(38)), kb(gsh[:]), k3(mug), ALU.subtract))
            link(TT(t(38), t(38), rw, ALU.mult))
            link(TT(k3(fin_d[:]), k3(t(38)), prm[:, 3, :].unsqueeze(2).broadcast_to([P, KC, NIMG]), ALU.add))

            def finish(s):
                for kbi in range(BK):
                    v = p2_bufs[s][:, kbi * ROW:(kbi + 1) * ROW]
                    ins = TS(v, v, fin_a[:, kbi:kbi + 1], fin_d[:, kbi:kbi + 1], ALU.mult, ALU.add)
                ins.then_inc(fin_done, 1)
            for s in range(SLOTS2):
                if s >= SLOTS:
                    dve.wait_ge(p2_loaded[s], 16)
                finish(s)
            with dve.Fori(1, P2_FULL + 1) as r:
                for s in range(SLOTS2):
                    dve.wait_ge(p2_loaded[s], r * 16 if s < SLOTS else r * 16 + 16)
                    finish(s)
            for s in range(P2_REST):
                dve.wait_ge(p2_loaded[s], 16 * (P2_FULL + 1))
                finish(s)


SMALL_GN0 = 20

_INS = ["x", "L0_conv_w_qkv", "L0_conv_w_out", "L0_conv_bias_table", "L1_conv_running_mean",
        "L1_conv_running_var", "L1_conv_weight", "L1_conv_bias", "L1_conv_source_rate"]
_OUT = ((4, 256, 128, 128), "float32")


def kernel(**inputs):
    import numpy as _np
    import concourse.bacc as _bacc
    from concourse import mybir as _mybir
    from concourse.bass_utils import run_bass_kernel_spmd as _run

    nc = _bacc.Bacc("TRN2", target_bir_lowering=False, num_devices=1)
    arrays, args = {}, []
    for name in _INS:
        a = _np.ascontiguousarray(inputs[name])
        if a.ndim < 1 or name.endswith("source_rate"):
            a = a.reshape(1, 1)
        arrays[f"in_{name}"] = a
        args.append(nc.dram_tensor(f"in_{name}", a.shape, _mybir.dt.from_np(a.dtype), kind="ExternalInput").ap())
    args.append(nc.dram_tensor("out_0", _OUT[0], _mybir.dt.from_np(_np.dtype(_OUT[1])), kind="ExternalOutput").ap())
    conv_preact_kernel(nc, *args)
    r = _run(nc, [arrays], core_ids=[0])
    return r.results[0]["out_0"]
```

```python
import concourse.bass as bass
from concourse import mybir
from contextlib import ExitStack


def conv_preact_kernel(nc, x, w_qkv, w_out, bias_table, running_mean, running_var, weight, bias,
                       source_rate, out):
    f32, f32r = mybir.dt.float32, mybir.dt.float32r
    ALU, ACT, AX = mybir.AluOpType, mybir.ActivationFunctionType, mybir.AxisListType

    NIMG, CH, H, W = x.shape
    P = 128
    KC = CH // P
    HEADS, WIN, MAXN = 4, 4, 5
    DH = CH // HEADS
    PIX = WIN * WIN
    TOK = NIMG * PIX
    HP = HEADS // 2
    STRIPS = H // WIN
    STEPS_PER_STRIP = 4
    WPS = W // WIN // STEPS_PER_STRIP
    WP = WPS // 2
    NT = WPS * TOK
    NSTEP = STRIPS * STEPS_PER_STRIP
    ROW = WIN * W
    STRIP = KC * NIMG * ROW
    SLOTS = 4
    SLOTS2 = SLOTS + 5
    BK = NIMG * KC
    HW = H * W
    NCHUNK = HW // 512
    GROUP = CH // 32
    GN_EPS, BN_EPS, CL_EPS = 1e-5, 1e-5, 1e-5
    QSCALE = float(DH) ** -0.5
    NREL = 2 * WIN - 1

    x_bk = x.rearrange("b (k p) h w -> (b k) p (h w)", p=P)
    x_strips = [x[:, k * P:(k + 1) * P, :, :].rearrange("b p (s r) w -> s p b (r w)", r=WIN)
                for k in range(KC)]
    out_strips = [out[:, k * P:(k + 1) * P, :, :].rearrange("b p (s r) w -> s p b (r w)", r=WIN)
                  for k in range(KC)]

    x1_dram = nc.dram_tensor("x1_strips", [STRIPS, P, STRIP], f32, kind="Internal").ap()
    rel_c = nc.dram_tensor("rel_c", [(2 * MAXN - 1) * NREL, PIX * HEADS], f32, kind="Internal").ap()
    rel_rc = nc.dram_tensor("rel_rc", [2 * MAXN - 1, PIX, PIX * HEADS], f32, kind="Internal").ap()

    ctx = ExitStack()
    with ctx:
        def sb(name, shape, dt=f32):
            return ctx.enter_context(nc.sbuf_tensor(name, shape, dt))

        def pb(name, shape):
            return ctx.enter_context(nc.psum_tensor(name, shape, f32))

        def sem(name):
            return ctx.enter_context(nc.semaphore(name))

        xs = sb("xs", [P, SLOTS, STRIP])
        xn = sb("xn", [P, 2, STRIP])
        xhi = [sb(f"xhi{i}", [P, KC, NT], f32r) for i in range(2)]
        xlo = [sb(f"xlo{i}", [P, KC, NT], f32r) for i in range(2)]
        q_sb = sb("q_sb", [P, HP, NT])
        kbd = sb("kbd", [P, HP, WPS, 2, TOK])
        v_all = sb("v_all", [P, STEPS_PER_STRIP, WP, CH])
        v_sb = [v_all[:, i, :, :] for i in range(STEPS_PER_STRIP)]
        prob_all = sb("prob_all", [P, 2, WP, HEADS, TOK])
        prob = [prob_all[:, i, :, :, :] for i in range(2)]
        ptbd = sb("ptbd", [P, WP, HP, 2, 2, TOK])
        ot_hi = sb("ot_hi", [P, HP, NT], f32r)
        ot_lo = sb("ot_lo", [P, HP, NT], f32r)
        wf = sb("wf", [P, KC, 4 * CH])
        whi = sb("whi", [P, KC, 4 * CH], f32r)
        wlo = sb("wlo", [P, KC, 4 * CH], f32r)
        bias_kh = sb("bias_kh", [P, TOK, HEADS])
        bias_sb = sb("bias_sb", [P, HEADS, TOK])
        ident = sb("ident", [P, P])
        gmat = sb("gmat", [P, P])
        ones = sb("ones", [P, P])
        stats = sb("stats", [P, BK, NCHUNK, 6])
        mv = sb("mv", [P, BK, 2])
        rmax = sb("rmax", [P, 2, WP * HEADS])
        rsum = sb("rsum", [P, 2, WP * HEADS])
        rinv = sb("rinv", [P, 2, WP * HEADS])
        gsc = sb("gsc", [P, BK])
        gsh = sb("gsh", [P, BK])
        fin_a = sb("fin_a", [P, BK])
        fin_d = sb("fin_d", [P, BK])
        prm = sb("prm", [P, 4, KC])
        rate = sb("rate", [P, 2])
        sc = sb("sc", [P, 40, 16])
        cube = sb("cube", [P, 2, 64])

        ps_a0 = pb("ps_a0", [P, 1024])
        ps_a1 = pb("ps_a1", [P, 1024])
        ps_b = pb("ps_b", [P, 1024])
        ps_c = pb("ps_c", [P, 1024])

        w_loaded, par_loaded = sem("w_loaded"), sem("par_loaded")
        relc_done, relrc_done, bias_loaded = sem("relc_done"), sem("relrc_done"), sem("bias_loaded")
        consts_ready, pads_ready = sem("consts_ready"), sem("pads_ready")
        w_hi_ready, w_lo_ready = sem("w_hi_ready"), sem("w_lo_ready")
        pool_chain = sem("pool_chain")
        p0_loaded = [sem(f"p0_loaded{i}") for i in range(SLOTS)]
        p0_stats = sem("p0_stats")
        small = sem("small")
        to_pe, from_pe = sem("to_pe"), sem("from_pe")
        to_act, from_act = sem("to_act"), sem("from_act")
        x_loaded = sem("x_loaded")
        xn_ready, xhi_ready, xlo_ready = sem("xn_ready"), sem("xhi_ready"), sem("xlo_ready")
        q_done, k_done, v_done = sem("q_done"), sem("k_done"), sem("v_done")
        s_done, pv_done, out_done = sem("s_done"), sem("pv_done"), sem("out_done")
        q_evac, k_evac, v_evac = sem("q_evac"), sem("k_evac"), sem("v_evac")
        biased, max_ready, shifted, exp_done = sem("biased"), sem("max_ready"), sem("shifted"), sem("exp_done")
        sum_ready, inv_ready, norm_done = sem("sum_ready"), sem("inv_ready"), sem("norm_done")
        pt_ready, o_evac, olo_ready, res_done = sem("pt_ready"), sem("o_evac"), sem("olo_ready"), sem("res_done")
        x1_stats, x1_stored = sem("x1_stats"), sem("x1_stored")
        p2_loaded = [sem(f"p2_loaded{i}") for i in range(SLOTS2)]
        p2_stored = [sem(f"p2_stored{i}") for i in range(SLOTS2)]
        fin_done = sem("fin_done")

        def steps(eng, body, peeled=1):
            def strip(i, first, last):
                for g in range(STEPS_PER_STRIP):
                    body(i, g, lambda lag, g=g: (not first or g >= lag) and (not last or g - lag < STEPS_PER_STRIP))
            for i in range(peeled):
                strip(i, i == 0, False)
            with eng.Fori(peeled, STRIPS - 1) as i:
                strip(i, False, False)
            strip(STRIPS - 1, False, True)
            for g in range(3):
                body(STRIPS, g, lambda lag, g=g: lag > g)

        def slot(eng, i, n):
            return i % n if isinstance(i, int) else eng.snap(i & (n - 1))

        def xs_at(s, k, lo, n):
            v = xs[:, s:s + 1, :] if isinstance(s, int) else xs[:, bass.ds(s, 1), :]
            v = v.rearrange("p a f -> p (a f)")
            return v[:, k * NIMG * ROW + lo:k * NIMG * ROW + lo + n]

        def xn_at(s):
            v = xn[:, s:s + 1, :] if isinstance(s, int) else xn[:, bass.ds(s, 1), :]
            return v.rearrange("p a f -> p (a f)").rearrange("p (k f) -> p k f", k=KC)

        HALF = STRIP // KC
        p2_bufs = [[xs[:, s, k * HALF:(k + 1) * HALF] for k in range(KC)] for s in range(SLOTS)]
        p2_bufs += [[xn[:, s, k * HALF:(k + 1) * HALF] for k in range(KC)] for s in range(2)]
        p2_bufs += [[v_all[:, 2 * k:2 * k + 2, :, :].rearrange("p i w c -> p (i w c)") for k in range(KC)],
                    [kbd[:].rearrange("p a w h t -> p (a w h t)"), ptbd[:].rearrange("p w a h v t -> p (w a h v t)")],
                    [prob_all[:].rearrange("p i w h t -> p (i w h t)"), wf[:].rearrange("p k n -> p (k n)")]]
        P2_FIRST = [STRIPS - SLOTS + s for s in range(SLOTS)] + list(range(SLOTS2 - SLOTS))
        P2_FULL, P2_REST = divmod(STRIPS - SLOTS2, SLOTS2)

        def p2_strip(r, s):
            return r * SLOTS2 + (s - SLOTS)

        block = ctx.enter_context(nc.Block())

        @block.sync
        def _(sp):
            def piece(t, q):
                return x_bk[t:t + 1, :, q * STRIP:(q + 1) * STRIP] if isinstance(t, int) else \
                    x_bk[bass.ds(t, 1), :, q * STRIP:(q + 1) * STRIP]
            for q in range(SLOTS):
                sp.dma_start(xs[:, q, :], piece(0, q).rearrange("a p f -> p (a f)")).then_inc(p0_loaded[q], 16)
            with sp.Fori(1, BK) as t:
                read = [sp.snap(t * SLOTS + (q + 1 - SLOTS)) for q in range(SLOTS)]
                for q in range(SLOTS):
                    sp.wait_ge(p0_stats, read[q])
                    sp.dma_start(xs[:, q, :], piece(t, q).rearrange("a p f -> p (a f)")).then_inc(p0_loaded[q], 16)

            sp.dma_start(wf[:, :, 0:3 * CH], w_qkv.rearrange("(k p) n -> p k n", p=P)).then_inc(w_loaded, 16)
            sp.dma_start(wf[:, :, 3 * CH:4 * CH], w_out.rearrange("(k p) n -> p k n", p=P)).then_inc(w_loaded, 16)

            def load(i, s):
                for k in range(KC):
                    src = x_strips[k][i:i + 1] if isinstance(i, int) else x_strips[k][bass.ds(i, 1)]
                    v = xs[:, s:s + 1, :] if isinstance(s, int) else xs[:, bass.ds(s, 1), :]
                    v = v.rearrange("p a f -> p (a f)")[:, k * NIMG * ROW:(k + 1) * NIMG * ROW]
                    sp.dma_start(v.rearrange("p (b f) -> p b f", b=NIMG),
                                 src.rearrange("a p b f -> p (a b) f")).then_inc(x_loaded, 16)

            for i in range(SLOTS - 1):
                sp.wait_ge(p0_stats, (BK - 1) * SLOTS + i + 1)
                if i:
                    sp.wait_ge(x_loaded, 32 * i)
                load(i, i)
            sp.wait_ge(p0_stats, BK * SLOTS)
            sp.wait_ge(x_loaded, 32 * (SLOTS - 1))
            load(SLOTS - 1, SLOTS - 1)

            def store(m, s):
                dst = x1_dram[m:m + 1] if isinstance(m, int) else x1_dram[bass.ds(m, 1)]
                v = xs[:, s:s + 1, :] if isinstance(s, int) else xs[:, bass.ds(s, 1), :]
                sp.dma_start(dst.rearrange("a p f -> p (a f)"), v.rearrange("p a f -> p (a f)")).then_inc(x1_stored, 16)

            with sp.Fori(1, STRIPS - SLOTS + 1) as i:
                s = slot(sp, i + (SLOTS - 1), SLOTS)
                before, ahead = sp.snap(i - 1), sp.snap(i + (SLOTS - 1))
                steps_before, stored, loaded = sp.snap(i * STEPS_PER_STRIP), sp.snap(i * 16), sp.snap(i * 32 + 32 * (SLOTS - 1))
                sp.wait_ge(res_done, steps_before)
                store(before, s)
                sp.wait_ge(x1_stats, stored)
                sp.wait_ge(x1_stored, stored)
                sp.wait_ge(x_loaded, loaded)
                load(ahead, s)

            def fetch(m, s):
                for k in range(KC):
                    src = x1_dram[m:m + 1] if isinstance(m, int) else x1_dram[bass.ds(m, 1)]
                    src = src.rearrange("a p f -> p (a f)")[:, k * HALF:(k + 1) * HALF]
                    sp.dma_start(p2_bufs[s][k], src).then_inc(p2_loaded[s], 16)

            sp.wait_ge(xlo_ready, NSTEP)
            sp.wait_ge(xhi_ready, NSTEP)
            sp.wait_ge(x1_stored, 16 * (STRIPS - SLOTS))
            for s in range(SLOTS, SLOTS2):
                if s == SLOTS + 2:
                    sp.wait_ge(pv_done, NSTEP)
                fetch(P2_FIRST[s], s)
            with sp.Fori(1, P2_FULL + 1) as r:
                strips = [sp.snap(p2_strip(r, s)) for s in range(SLOTS2)]
                written = sp.snap(r * 32)
                for s in range(SLOTS2):
                    sp.wait_ge(p2_stored[s], written)
                    fetch(strips[s], s)
            for s in range(P2_REST):
                sp.wait_ge(p2_stored[s], 32 * (P2_FULL + 1))
                fetch(p2_strip(P2_FULL + 1, s), s)

        @block.gpsimd
        def _(pool):
            pool.memset(ident[:], 0.0).then_inc(pool_chain, 1)
            pool.memset(gmat[:], 1.0 / GROUP).then_inc(pool_chain, 1)
            pool.memset(ones[:], 1.0).then_inc(consts_ready, 1)
            pool.wait_ge(pool_chain, 2)
            pool.affine_select(out=ident[:], in_=ident[:], compare_op=ALU.not_equal, fill=1.0, base=0,
                               pattern=[[-1, P]], channel_multiplier=1).then_inc(consts_ready, 1)
            g3 = gmat[:].rearrange("p (g j) -> p g j", j=GROUP)
            pool.affine_select(out=g3, in_=g3, compare_op=ALU.is_ge, fill=0.0, base=0,
                               pattern=[[-GROUP, P // GROUP], [0, GROUP]], channel_multiplier=1).then_inc(pool_chain, 1)
            pool.wait_ge(pool_chain, 3)
            pool.affine_select(out=g3, in_=g3, compare_op=ALU.is_ge, fill=0.0, base=GROUP - 1,
                               pattern=[[GROUP, P // GROUP], [0, GROUP]], channel_multiplier=-1).then_inc(consts_ready, 1)
            pool.memset(kbd[:], 0.0).then_inc(pads_ready, 1)
            pool.memset(ptbd[:], 0.0).then_inc(pads_ready, 1)
            pool.wait_ge(w_hi_ready, 1)
            pool.tensor_tensor(wlo[:], wf[:], whi[:], ALU.subtract).then_inc(w_lo_ready, 1)

            def low_part(i, g, m):
                src = xn_at(slot(pool, i, 2))[:, :, g * NT:(g + 1) * NT]
                pool.wait_ge(xhi_ready, m + 1)
                pool.tensor_tensor(xlo[g % 2][:], src, xhi[g % 2][:], ALU.subtract).then_inc(xlo_ready, 1)

            low_part(0, 0, 0)

            def body(i, g, ok):
                n = i * STEPS_PER_STRIP + g
                if ok(1):
                    pool.wait_ge(max_ready, n)
                    j = (g - 1) % 2
                    p3 = prob[j].rearrange("p w h t -> p (w h) t")
                    pool.tensor_tensor(p3, p3, rmax[:, j, :].unsqueeze(2).broadcast_to([P, WP * HEADS, TOK]),
                                       ALU.subtract).then_inc(shifted, 1)
                if ok(-1):
                    pool_i, pool_g = (i, g + 1) if g + 1 < STEPS_PER_STRIP else (i + 1, 0)
                    low_part(pool_i, pool_g, n + 1)
                if ok(1):
                    pool.wait_ge(inv_ready, n)
                    pool.tensor_tensor(p3, p3, rinv[:, j, :].unsqueeze(2).broadcast_to([P, WP * HEADS, TOK]),
                                       ALU.mult).then_inc(norm_done, 1)

            steps(pool, body)

        @block.scalar
        def _(act):
            for n, v in enumerate((running_mean, running_var, weight, bias)):
                for k in range(KC):
                    act.dma_start(prm[:, n, k:k + 1], v[k * P:(k + 1) * P].unsqueeze(1)).then_inc(par_loaded, 16)
            act.dma_start(rate[:, 0:1], source_rate.broadcast_to([P, 1])).then_inc(par_loaded, 16)

            TE, F = HEADS, PIX * HEADS
            for c1 in range(WIN):
                src = bass.AP(bias_table.tensor, (c1 + WIN - 1) * TE,
                              [[NREL * TE, (2 * MAXN - 1) * NREL], [-TE, WIN], [1, TE]])
                act.dma_start(rel_c[:, c1 * WIN * TE:(c1 + 1) * WIN * TE].rearrange("a (c h) -> a c h", h=TE), src)\
                    .then_inc(relc_done, 16)
            act.wait_ge(relc_done, 16 * WIN)
            for r1 in range(WIN):
                for c1 in range(WIN):
                    src = bass.AP(rel_c.tensor, (r1 + WIN - 1) * F + c1 * WIN * TE,
                                  [[NREL * F, 2 * MAXN - 1], [-F, WIN], [1, WIN * TE]])
                    act.dma_start(rel_rc[:, r1 * WIN + c1, :].rearrange("a (r e) -> a r e", r=WIN), src)\
                        .then_inc(relrc_done, 16)
            act.wait_ge(relrc_done, 16 * PIX)
            for half in range(2):
                for f1 in range(NIMG):
                    src = bass.AP(rel_rc.tensor, (f1 + MAXN - 1) * PIX * F, [[F, PIX], [-PIX * F, NIMG], [1, F]])
                    q0 = half * TOK + f1 * PIX
                    act.dma_start(bias_kh[q0:q0 + PIX].rearrange("p (f t) h -> p f (t h)", f=NIMG), src)\
                        .then_inc(bias_loaded, 16)

            act.wait_ge(w_loaded, 32)
            act.activation(whi[:], wf[:], ACT.Copy).then_inc(w_hi_ready, 1)

            act.wait_ge(to_act, 1)
            act.activation(sc[:, 1, 0:BK], sc[:, 0, 0:BK], ACT.Sqrt).then_inc(from_act, 1)

            def normalise(i, piece):
                k, b = divmod(piece, NIMG)
                src = xs_at(slot(act, i, SLOTS), k, b * ROW, ROW).rearrange("p (r w c) -> p w r c", r=WIN, c=WIN)
                dst = xn_at(slot(act, i, 2))[:, k, :].rearrange("p (w b r c) -> p b w r c", b=NIMG, r=WIN, c=WIN)[:, b]
                j = b * KC + k
                act.activation(dst, src, ACT.Identity, bias=gsh[:, j:j + 1], scale=gsc[:, j:j + 1]).then_inc(xn_ready, 1)

            act.wait_ge(small, SMALL_GN0)
            act.wait_ge(x_loaded, 32)
            for piece in range(BK):
                normalise(0, piece)

            def high_part(i, g):
                src = xn_at(slot(act, i, 2))[:, :, g * NT:(g + 1) * NT]
                act.activation(xhi[g % 2][:], src, ACT.Copy).then_inc(xhi_ready, 1)

            act.wait_ge(xn_ready, BK)
            high_part(0, 0)
            act.wait_ge(pads_ready, 2)

            def body(i, g, ok):
                n = i * STEPS_PER_STRIP + g
                if ok(-STEPS_PER_STRIP):
                    if g == 0:
                        act.wait_ge(x_loaded, i * 32 + 64)
                        if not isinstance(i, int) or i > 0:
                            act.wait_ge(xhi_ready, i * STEPS_PER_STRIP)
                            act.wait_ge(xlo_ready, i * STEPS_PER_STRIP)
                    nxt = i + 1 if isinstance(i, int) else act.snap(i + 1)
                    normalise(nxt, 2 * g)
                    normalise(nxt, 2 * g + 1)
                if ok(-1):
                    if g == STEPS_PER_STRIP - 1:
                        act.wait_ge(xn_ready, i * BK + 2 * BK)
                    if ok(1):
                        act.wait_ge(v_done, n)
                        act.wait_ge(xlo_ready, n)
                if ok(0):
                    act.wait_ge(q_done, n + 1)
                    act.activation(q_sb[:].rearrange("p a t -> p (a t)"), ps_a0[:], ACT.Copy, scale=QSCALE).then_inc(q_evac, 1)
                    if ok(-1):
                        if g + 1 < STEPS_PER_STRIP:
                            high_part(i, g + 1)
                        else:
                            high_part(nxt, 0)
                    act.wait_ge(k_done, n + 1)
                    for hh in range(2):
                        rows = slice(hh * DH, (hh + 1) * DH)
                        ins = act.activation(kbd[rows, :, :, hh, :].rearrange("p a w t -> p (a w) t"),
                                             ps_a1[rows, :].rearrange("p (aw t) -> p aw t", t=TOK), ACT.Copy)
                    ins.then_inc(k_evac, 1)
                if ok(1):
                    act.wait_ge(shifted, n)
                    p2 = prob[(g - 1) % 2].rearrange("p w h t -> p (w h t)")
                    act.activation(p2, p2, ACT.Exp).then_inc(exp_done, 1)
                if ok(0):
                    act.wait_ge(v_done, n + 1)
                    act.activation(v_sb[g].rearrange("p w c -> p (w c)"), ps_a0[:], ACT.Copy).then_inc(v_evac, 1)
                if ok(2):
                    act.wait_ge(pv_done, n - 1)
                    act.activation(ot_hi[:].rearrange("p a t -> p (a t)"), ps_c[:], ACT.Copy).then_inc(o_evac, 1)

            steps(act, body)

            for r in range(2):
                act.wait_ge(to_act, 2 + r)
                act.activation(sc[:, 1, 0:BK], sc[:, 0, 0:BK], ACT.Sqrt).then_inc(from_act, 1)
            act.wait_ge(to_act, 4)
            act.activation(sc[:, 1, 0:BK], sc[:, 0, 0:BK], ACT.Sqrt).then_inc(from_act, 1)

            def store(m, s, count):
                act.wait_ge(fin_done, count)
                for k in range(KC):
                    dst = out_strips[k][m:m + 1] if isinstance(m, int) else out_strips[k][bass.ds(m, 1)]
                    act.dma_start(dst.rearrange("a p b f -> p (a b) f"),
                                  p2_bufs[s][k].rearrange("p (b f) -> p b f", b=NIMG))\
                        .then_inc(p2_stored[s], 16)
            for s in range(SLOTS2):
                store(P2_FIRST[s], s, s + 1)
            with act.Fori(1, P2_FULL + 1) as r:
                for s in range(SLOTS2):
                    store(act.snap(p2_strip(r, s)), s, r * SLOTS2 + (s + 1))
            for s in range(P2_REST):
                store(p2_strip(P2_FULL + 1, s), s, (P2_FULL + 1) * SLOTS2 + s + 1)
            for s in range(SLOTS2):
                act.wait_ge(p2_stored[s], 32 * (P2_FULL + 1 + (s < P2_REST)))

        @block.tensor
        def _(pe):
            def small_mm(n, dst, lhsT, parts):
                pe.wait_ge(to_pe, n)
                for j, r in enumerate(parts):
                    ins = pe.matmul(dst, lhsT, r, start=(j == 0), stop=(j == len(parts) - 1))
                ins.then_inc(from_pe, 1)

            pe.wait_ge(consts_ready, 3)
            pe.wait_ge(w_lo_ready, 1)
            small_mm(1, ps_b[:, 0:BK], gmat[:], [sc[:, 2, 0:BK]])
            small_mm(2, ps_b[:, 0:BK], gmat[:], [sc[:, 3, 0:BK]])

            def body(i, g, ok):
                n = i * STEPS_PER_STRIP + g
                hi, lo = xhi[g % 2], xlo[g % 2]

                def project_qk(ps, col0):
                    for a in range(HP):
                        cols = slice(col0 + a * P, col0 + (a + 1) * P)
                        terms = [(w[:, k, cols], t[:, k, :]) for k in range(KC) for w, t in ((whi, hi), (whi, lo), (wlo, hi))]
                        for j, (w, t) in enumerate(terms):
                            ins = pe.matmul(ps[:, a * NT:(a + 1) * NT], w, t, start=(j == 0), stop=(j == len(terms) - 1))
                    return ins

                if ok(1):
                    pe.wait_ge(q_evac, n)
                    pe.wait_ge(k_evac, n)
                    if ok(4):
                        pe.wait_ge(res_done, n - 3)
                    elif ok(2):
                        pe.wait_ge(biased, n - 1)
                    for w in range(WPS):
                        rows = slice(w % 2 * TOK, (w % 2 + 1) * TOK)
                        for a in range(HP):
                            c = w // 2 * HEADS * TOK + a * 2 * TOK
                            ins = pe.matmul(ps_b[rows, c:c + 2 * TOK], q_sb[:, a, w * TOK:(w + 1) * TOK],
                                            kbd[:, a, w, :, :].rearrange("p h t -> p (h t)"), start=True, stop=True)
                    ins.then_inc(s_done, 1)
                if ok(0):
                    pe.wait_ge(xhi_ready, n + 1)
                    pe.wait_ge(xlo_ready, n + 1)
                    if ok(1):
                        pe.wait_ge(v_evac, n)
                    project_qk(ps_a0, 0).then_inc(q_done, 1)
                    if ok(1):
                        pe.wait_ge(k_evac, n)
                    project_qk(ps_a1, CH).then_inc(k_done, 1)
                if ok(0):
                    pe.wait_ge(q_evac, n + 1)
                    for w in range(WP):
                        toks = slice(w * 2 * TOK, (w + 1) * 2 * TOK)
                        terms = [(t[:, k, toks], wt[:, k, 2 * CH:3 * CH]) for k in range(KC) for t, wt in ((hi, whi), (hi, wlo), (lo, whi))]
                        for j, (t, wt) in enumerate(terms):
                            ins = pe.matmul(ps_a0[:, w * CH:(w + 1) * CH], t, wt, start=(j == 0), stop=(j == len(terms) - 1))
                    ins.then_inc(v_done, 1)
                if ok(3):
                    pe.wait_ge(olo_ready, n - 2)
                    if ok(1):
                        pe.wait_ge(biased, n)
                    else:
                        pe.wait_ge(res_done, n - 3)
                    for m in range(KC):
                        terms = [(w[:, k, 3 * CH + m * P:3 * CH + (m + 1) * P], t[:, k, :]) for k in range(KC)
                                 for w, t in ((whi, ot_hi), (whi, ot_lo), (wlo, ot_hi))]
                        for j, (w, t) in enumerate(terms):
                            ins = pe.matmul(ps_b[:, m * NT:(m + 1) * NT], w, t, start=(j == 0), stop=(j == len(terms) - 1))
                    ins.then_inc(out_done, 1)
                if ok(2):
                    pe.wait_ge(pt_ready, n - 1)
                    pe.wait_ge(v_evac, n - 1)
                    for w in range(WP):
                        for a in range(HP):
                            for hh in range(2):
                                h = 2 * a + hh
                                ins = pe.matmul(ps_c[hh * DH:(hh + 1) * DH, a * NT + w * P:a * NT + (w + 1) * P],
                                                v_sb[(g - 2) % 4][:, w, h * DH:(h + 1) * DH],
                                                ptbd[:, w, a, hh, :, :].rearrange("p v t -> p (v t)"), start=True, stop=True)
                    ins.then_inc(pv_done, 1)

            steps(pe, body)
            small_mm(3, ps_b[:, 0:BK], gmat[:], [sc[:, 2, 0:BK]])
            small_mm(4, ps_b[:, 0:BK], gmat[:], [sc[:, 3, 0:BK]])
            small_mm(5, ps_b[:, 0:16], ones[:], [sc[:, 10, 0:16], sc[:, 11, 0:16]])

        @block.vector
        def _(dve):
            chain = [0]

            def link(ins):
                chain[0] += 1
                ins.then_inc(small, 1)
                dve.wait_ge(small, chain[0])

            asks = {"pe": 0, "act": 0}

            def ask(who):
                asks[who] += 1
                there, back = (to_pe, from_pe) if who == "pe" else (to_act, from_act)
                dve.sem_inc(there, 1)
                dve.wait_ge(back, asks[who])

            TT, TS, STT = dve.tensor_tensor, dve.tensor_scalar, dve.scalar_tensor_tensor

            def rsqrt(dst, v, n):
                ask("act")
                y, t = sc[:, 1, 0:n], sc[:, 4, 0:n]
                link(dve.reciprocal(y, sc[:, 1, 0:n]))
                link(TT(t, y, y, ALU.mult))
                link(TT(t, t, v, ALU.mult))
                link(TS(t, t, -0.5, 1.5, ALU.mult, ALU.add))
                link(TT(dst, y, t, ALU.mult))

            def aggregate(rows):
                for j in rows:
                    ins = dve.bn_aggr(mv[:, j, :], stats[:, j, :, :].rearrange("p n s -> p (n s)"))
                return ins

            def group_norm():
                mean, var = mv[:, :, 0], mv[:, :, 1]
                link(dve.tensor_copy(sc[:, 2, 0:BK], mean))
                ask("pe")
                gm, t = sc[:, 5, 0:BK], sc[:, 6, 0:BK]
                link(dve.tensor_copy(gm, ps_b[:, 0:BK]))
                link(TT(t, sc[:, 2, 0:BK], gm, ALU.subtract))
                link(TT(t, t, t, ALU.mult))
                link(TT(sc[:, 3, 0:BK], t, var, ALU.add))
                ask("pe")
                link(TS(sc[:, 0, 0:BK], ps_b[:, 0:BK], GN_EPS, None, ALU.add))
                rsqrt(gsc[:], sc[:, 0, 0:BK], BK)
                link(STT(out=gsh[:], in0=gm, scalar=-1.0, in1=gsc[:], op0=ALU.mult, op1=ALU.mult))

            def piece_stats(t, q):
                for j in range(STRIP // 512):
                    c = q * (STRIP // 512) + j
                    dst = stats[:, t:t + 1, c, :] if isinstance(t, int) else stats[:, bass.ds(t, 1), c, :]
                    ins = dve.bn_stats(dst.rearrange("p a s -> p (a s)"), xs[:, q, j * 512:(j + 1) * 512])
                ins.then_inc(p0_stats, 1)
            with dve.Fori(0, BK - 1) as t:
                for q in range(SLOTS):
                    dve.wait_ge(p0_loaded[q], t * 16 + 16)
                    piece_stats(t, q)
            dve.wait_ge(p0_stats, (BK - 1) * SLOTS)
            aggregate(range(BK - 1))
            for q in range(SLOTS):
                dve.wait_ge(p0_loaded[q], BK * 16)
                piece_stats(BK - 1, q)
            dve.wait_ge(p0_stats, BK * SLOTS)
            link(aggregate([BK - 1]))
            group_norm()
            assert chain[0] == SMALL_GN0, chain[0]
            dve.wait_ge(bias_loaded, 16 * 8)
            link(dve.tensor_copy(bias_sb[:], bias_kh[:].rearrange("p t h -> p h t")))

            def t(n, w=BK):
                return sc[:, n, 0:w]

            def kb(ap):
                return ap.rearrange("p (b k) -> p k b", k=KC)

            def sq(ap):
                return ap.rearrange("p (i j) -> p i j", j=NIMG)

            def over_i(ap):
                return ap.unsqueeze(2).broadcast_to([P, NIMG, NIMG])

            def over_j(ap):
                return ap.unsqueeze(1).broadcast_to([P, NIMG, NIMG])

            idx, eye, mixed = t(14, NIMG), t(15, 16), t(35, 4)
            for b in range(NIMG):
                link(dve.memset(sc[:, 14, b:b + 1], float(b - NIMG)))
            link(TT(sq(eye), over_i(idx), over_j(idx), ALU.is_equal))
            dve.wait_ge(par_loaded, 16 * (1 + 4 * KC))
            link(TS(rate[:, 0:1], rate[:, 0:1], 0.0, 1.0, ALU.max, ALU.min))
            link(TS(rate[:, 1:2], rate[:, 0:1], -1.0, 1.0, ALU.mult, ALU.add))
            link(TS(mixed, prm[:, 0:2, :].rearrange("p a k -> p (a k)"), rate[:, 0:1], None, ALU.mult))

            def strip_stats(m, pieces):
                s = slot(dve, m, SLOTS)
                for piece in pieces:
                    k, b = divmod(piece, NIMG)
                    dst = stats[:, b * KC + k, m:m + 1, :] if isinstance(m, int) else stats[:, b * KC + k, bass.ds(m, 1), :]
                    ins = dve.bn_stats(dst.rearrange("p a s -> p (a s)"), xs_at(s, k, b * ROW, ROW))
                if piece == BK - 1:
                    ins.then_inc(x1_stats, 16)

            def transpose_probs(pr):
                B = TOK // 2
                for v in range(2):
                    for qh in range(2):
                        for kh in range(2):
                            ins = dve.transpose(
                                ptbd[v * TOK + kh * B:v * TOK + (kh + 1) * B, :, :, :, v, qh * B:(qh + 1) * B]
                                .rearrange("p w a h t -> p (w a h) t"),
                                pr[v * TOK + qh * B:v * TOK + (qh + 1) * B, :, :, kh * B:(kh + 1) * B]
                                .rearrange("p w h t -> p (w h) t"))
                return ins

            dve.wait_ge(pads_ready, 2)

            def body(i, g, ok):
                n = i * STEPS_PER_STRIP + g
                j = (g - 1) % 2
                p3 = prob[j].rearrange("p w h t -> p (w h) t")
                if ok(3):
                    dve.wait_ge(o_evac, n - 2)
                    TT(ot_lo[:].rearrange("p a t -> p (a t)"), ps_c[:], ot_hi[:].rearrange("p a t -> p (a t)"),
                       ALU.subtract).then_inc(olo_ready, 1)
                if ok(1):
                    dve.wait_ge(s_done, n)
                    TT(prob[j].rearrange("p w h t -> p w (h t)"), ps_b[:].rearrange("p (w f) -> p w f", w=WP),
                       bias_sb[:].rearrange("p h t -> p (h t)").unsqueeze(1).broadcast_to([P, WP, HEADS * TOK]),
                       ALU.add).then_inc(biased, 1)
                    dve.wait_ge(biased, n)
                    dve.tensor_reduce(rmax[:, j, :], p3, AX.X, ALU.max).then_inc(max_ready, 1)
                if ok(2):
                    dve.wait_ge(norm_done, n - 1)
                    if ok(3):
                        dve.wait_ge(pv_done, n - 2)
                    transpose_probs(prob[g % 2]).then_inc(pt_ready, 1)
                if ok(1):
                    dve.wait_ge(exp_done, n)
                    dve.tensor_reduce(rsum[:, j, :], p3, AX.X, ALU.add).then_inc(sum_ready, 1)
                    dve.wait_ge(sum_ready, n)
                    dve.reciprocal(rinv[:, j, :], rsum[:, j, :]).then_inc(inv_ready, 1)
                if ok(3):
                    dve.wait_ge(out_done, n - 2)
                    sg = (g - 3) % 4
                    si = i if g == 3 else (i - 1 if isinstance(i, int) else dve.snap(i - 1))
                    s = slot(dve, si, SLOTS)
                    for m in range(KC):
                        v = xs_at(s, m, 0, NIMG * ROW).rearrange("p (br w) -> p br w", w=W)
                        v = v[:, :, sg * WPS * WIN:(sg + 1) * WPS * WIN].rearrange("p br (j c) -> p br j c", c=WIN)
                        o = ps_b[:, m * NT:(m + 1) * NT].rearrange("p (j br c) -> p br j c", br=NIMG * WIN, c=WIN)
                        ins = TT(v, o, v, ALU.add)
                    ins.then_inc(res_done, 1)
                m = (i - 1 if g >= 2 else i - 2) if isinstance(i, int) else dve.snap(i - 1 if g >= 2 else i - 2)
                if not isinstance(m, int) or m >= 0:
                    if g == 2:
                        dve.wait_ge(res_done, i * STEPS_PER_STRIP)
                    p = (g - 2) % STEPS_PER_STRIP
                    if isinstance(i, int) and i == STRIPS and g == 2:
                        strip_stats(m, range(BK))
                    else:
                        strip_stats(m, (2 * p, 2 * p + 1))

            steps(dve, body, peeled=2)

            dve.wait_ge(x1_stats, 16 * STRIPS)
            link(aggregate(range(BK)))
            group_norm()

            mu, sg2 = t(7), t(8)
            link(TT(mu, mv[:, :, 0], sc[:, 5, 0:BK], ALU.subtract))
            link(TT(mu, mu, gsc[:], ALU.mult))
            link(TT(sg2, mv[:, :, 1], gsc[:], ALU.mult))
            link(TT(sg2, sg2, gsc[:], ALU.mult))
            link(TS(sg2, sg2, float(HW) / (HW - 1), None, ALU.mult))
            for k in range(KC):
                m_k = kb(mu)[:, k, :]
                link(TT(t(10 + k, 16).rearrange("p (i j) -> p i j", j=NIMG), m_k.unsqueeze(2).broadcast_to([P, NIMG, NIMG]),
                        m_k.unsqueeze(1).broadcast_to([P, NIMG, NIMG]), ALU.mult))
            ask("pe")
            gram = t(12, 16)
            link(dve.tensor_copy(gram, ps_b[:, 0:16]))
            link(dve.memset(sc[:, 0, 0:BK], 1.0))
            link(dve.tensor_copy(sc[:, 0, 0:NIMG], gram[:, 0:16:NIMG + 1]))
            rn = t(13, BK)
            rsqrt(rn, sc[:, 0, 0:BK], BK)

            dist = t(16, 16)
            link(TT(sq(dist), sq(gram), over_i(rn[:, 0:NIMG]), ALU.mult))
            link(TT(sq(dist), sq(dist), over_j(rn[:, 0:NIMG]), ALU.mult))
            link(TS(dist, dist, -1.0, 1.0, ALU.mult, ALU.add))
            link(STT(out=dist, in0=eye, scalar=1e30, in1=dist, op0=ALU.mult, op1=ALU.add))
            dmin, cand, nn = t(17, NIMG), t(18, 16), t(19, NIMG)
            link(dve.tensor_reduce(dmin, sq(dist), AX.X, ALU.min))
            link(TT(sq(cand), sq(dist), over_i(dmin), ALU.is_equal))

            def masked_min(dst, mask, values):
                link(TT(sq(t(21, 16)), sq(mask), over_j(values), ALU.mult))
                link(dve.tensor_reduce(dst, sq(t(21, 16)), AX.X, ALU.min))

            masked_min(nn, cand, idx)
            nbr, adj = t(22, 16), t(23, 16)
            link(TT(sq(nbr), over_i(nn), over_j(idx), ALU.is_equal))
            link(TT(nbr, nbr, eye, ALU.add))
            c3 = cube[:, 0, :].rearrange("p (i j m) -> p i j m", j=NIMG, m=NIMG)
            link(TT(c3, sq(nbr).unsqueeze(2).broadcast_to([P, NIMG, NIMG, NIMG]),
                    sq(nbr).unsqueeze(1).broadcast_to([P, NIMG, NIMG, NIMG]), ALU.mult))
            link(dve.tensor_reduce(sq(adj), c3, AX.X, ALU.add))
            link(TS(adj, adj, 0.0, None, ALU.is_gt))
            link(STT(out=t(24, 16), in0=eye, scalar=-1.0, in1=adj, op0=ALU.mult, op1=ALU.add))
            link(TS(adj, t(24, 16), 0.0, None, ALU.is_gt))
            lab, near = t(25, NIMG), t(26, NIMG)
            link(dve.tensor_copy(lab, idx))
            for _ in range(NIMG - 1):
                masked_min(near, adj, lab)
                link(TT(lab, lab, near, ALU.min))
            oh, ohT, den = t(27, 16), t(28, 16), t(29, NIMG)
            link(TT(sq(oh), over_i(lab), over_j(idx), ALU.is_equal))
            link(dve.tensor_copy(sq(ohT), oh.rearrange("p (i l) -> p l i", l=NIMG)))
            link(dve.tensor_reduce(den, sq(ohT), AX.X, ALU.add))
            link(TS(den, den, CL_EPS, None, ALU.add))
            rden = t(39, NIMG)
            link(dve.reciprocal(rden, den))

            KLI = [P, KC, NIMG, NIMG]
            c4 = [cube[:, c, 0:32].rearrange("p (k l i) -> p k l i", k=KC, l=NIMG) for c in range(2)]

            def k3(ap):
                return ap.rearrange("p (k l) -> p k l", k=KC)

            def weighted(dst, vals):
                link(TT(c4[1], sq(ohT).unsqueeze(1).broadcast_to(KLI), vals, ALU.mult))
                link(dve.tensor_reduce(k3(dst), c4[1], AX.X, ALU.add))
                link(TT(k3(dst), k3(dst), rden.unsqueeze(1).broadcast_to([P, KC, NIMG]), ALU.mult))

            cm, cs, cd = t(30), t(31), t(32)
            weighted(cm, kb(mu).unsqueeze(2).broadcast_to(KLI))
            weighted(cs, kb(sg2).unsqueeze(2).broadcast_to(KLI))
            link(TT(c4[0], kb(mu).unsqueeze(2).broadcast_to(KLI), k3(cm).unsqueeze(3).broadcast_to(KLI), ALU.subtract))
            link(TT(c4[0], c4[0], c4[0], ALU.mult))
            weighted(cd, c4[0])
            link(TT(cs, cs, cd, ALU.add))

            def of_image(dst, per_cluster):
                link(TT(c4[1], sq(oh).unsqueeze(1).broadcast_to(KLI), k3(per_cluster).unsqueeze(2).broadcast_to(KLI), ALU.mult))
                link(dve.tensor_reduce(k3(dst), c4[1], AX.X, ALU.add))

            mug, sgg = t(33), t(34)
            of_image(mug, cm)
            of_image(sgg, cs)
            for n, v in enumerate((mug, sgg)):
                link(STT(out=k3(v), in0=k3(v), scalar=rate[:, 1:2], in1=mixed[:, n * KC:(n + 1) * KC].unsqueeze(2).broadcast_to([P, KC, NIMG]),
                         op0=ALU.mult, op1=ALU.add))
            link(TS(sc[:, 0, 0:BK], sgg, BN_EPS, None, ALU.add))
            rw = t(36)
            rsqrt(rw, sc[:, 0, 0:BK], BK)
            link(TT(k3(rw), k3(rw), prm[:, 2, :].unsqueeze(2).broadcast_to([P, KC, NIMG]), ALU.mult))
            link(TT(k3(t(37)), k3(rw), kb(gsc[:]), ALU.mult))
            link(TS(fin_a[:], t(37), 1.0, None, ALU.add))
            link(TT(k3(t(38)), kb(gsh[:]), k3(mug), ALU.subtract))
            link(TT(t(38), t(38), rw, ALU.mult))
            link(TT(k3(fin_d[:]), k3(t(38)), prm[:, 3, :].unsqueeze(2).broadcast_to([P, KC, NIMG]), ALU.add))

            def finish(s):
                for k in range(KC):
                    for b in range(NIMG):
                        v, j = p2_bufs[s][k][:, b * ROW:(b + 1) * ROW], k * NIMG + b
                        ins = TS(v, v, fin_a[:, j:j + 1], fin_d[:, j:j + 1], ALU.mult, ALU.add)
                ins.then_inc(fin_done, 1)
            for s in range(SLOTS2):
                if s >= SLOTS:
                    dve.wait_ge(p2_loaded[s], 32)
                finish(s)
            with dve.Fori(1, P2_FULL + 1) as r:
                for s in range(SLOTS2):
                    dve.wait_ge(p2_loaded[s], r * 32 if s < SLOTS else r * 32 + 32)
                    finish(s)
            for s in range(P2_REST):
                dve.wait_ge(p2_loaded[s], 32 * (P2_FULL + 1 + (s >= SLOTS)))
                finish(s)


SMALL_GN0 = 13

_INS = ["x", "L0_conv_w_qkv", "L0_conv_w_out", "L0_conv_bias_table", "L1_conv_running_mean",
        "L1_conv_running_var", "L1_conv_weight", "L1_conv_bias", "L1_conv_source_rate"]
_OUT = ((4, 256, 128, 128), "float32")


def kernel(**inputs):
    import numpy as _np
    import concourse.bacc as _bacc
    from concourse import mybir as _mybir
    from concourse.bass_utils import run_bass_kernel_spmd as _run

    nc = _bacc.Bacc("TRN2", target_bir_lowering=False, num_devices=1)
    arrays, args = {}, []
    for name in _INS:
        a = _np.ascontiguousarray(inputs[name])
        if a.ndim < 1 or name.endswith("source_rate"):
            a = a.reshape(1, 1)
        arrays[f"in_{name}"] = a
        args.append(nc.dram_tensor(f"in_{name}", a.shape, _mybir.dt.from_np(a.dtype), kind="ExternalInput").ap())
    args.append(nc.dram_tensor("out_0", _OUT[0], _mybir.dt.from_np(_np.dtype(_OUT[1])), kind="ExternalOutput").ap())
    conv_preact_kernel(nc, *args)
    r = _run(nc, [arrays], core_ids=[0])
    return r.results[0]["out_0"]
```

```python
import concourse.bass as bass
from concourse import mybir
from contextlib import ExitStack


def conv_preact_kernel(nc, x, w_qkv, w_out, bias_table, running_mean, running_var, weight, bias,
                       source_rate, out):
    f32, f32r = mybir.dt.float32, mybir.dt.float32r
    ALU, ACT, AX = mybir.AluOpType, mybir.ActivationFunctionType, mybir.AxisListType

    NIMG, CH, H, W = x.shape
    P = 128
    KC = CH // P
    HEADS, WIN, MAXN = 4, 4, 5
    DH = CH // HEADS
    PIX = WIN * WIN
    TOK = NIMG * PIX
    HP = HEADS // 2
    STRIPS = H // WIN
    STEPS_PER_STRIP = 4
    WPS = W // WIN // STEPS_PER_STRIP
    WP = WPS // 2
    NT = WPS * TOK
    NSTEP = STRIPS * STEPS_PER_STRIP
    ROW = WIN * W
    STRIP = KC * NIMG * ROW
    SLOTS = 4
    SLOTS2 = SLOTS + 8
    BK = NIMG * KC
    HW = H * W
    NCHUNK = HW // 512
    GROUP = CH // 32
    GN_EPS, BN_EPS, CL_EPS = 1e-5, 1e-5, 1e-5
    QSCALE = float(DH) ** -0.5
    NREL = 2 * WIN - 1

    x_bk = x.rearrange("b (k p) h w -> (b k) p (h w)", p=P)
    x_strips = [x[:, k * P:(k + 1) * P, :, :].rearrange("b p (s r) w -> s p b (r w)", r=WIN)
                for k in range(KC)]
    out_strips = [out[:, k * P:(k + 1) * P, :, :].rearrange("b p (s r) w -> s p b (r w)", r=WIN)
                  for k in range(KC)]

    x1_dram = nc.dram_tensor("x1_strips", [STRIPS, P, STRIP], f32, kind="Internal").ap()
    rel_c = nc.dram_tensor("rel_c", [(2 * MAXN - 1) * NREL, PIX * HEADS], f32, kind="Internal").ap()
    rel_rc = nc.dram_tensor("rel_rc", [2 * MAXN - 1, PIX, PIX * HEADS], f32, kind="Internal").ap()

    ctx = ExitStack()
    with ctx:
        def sb(name, shape, dt=f32):
            return ctx.enter_context(nc.sbuf_tensor(name, shape, dt))

        def pb(name, shape):
            return ctx.enter_context(nc.psum_tensor(name, shape, f32))

        def sem(name):
            return ctx.enter_context(nc.semaphore(name))

        xs = sb("xs", [P, SLOTS, STRIP])
        xn = sb("xn", [P, 2, STRIP])
        q_sb = sb("q_sb", [P, HP, NT])
        kbd = sb("kbd", [P, HP, WPS, 2, TOK])
        v_all = sb("v_all", [P, STEPS_PER_STRIP, WP, CH])
        v_sb = [v_all[:, i, :, :] for i in range(STEPS_PER_STRIP)]
        prob_all = sb("prob_all", [P, 2, WP, HEADS, TOK])
        prob = [prob_all[:, i, :, :, :] for i in range(2)]
        ptbd = sb("ptbd", [P, WP, HP, 2, 2, TOK])
        spare = sb("spare", [P, STRIP // KC])
        wf = sb("wf", [P, KC, 4 * CH])
        bias_kh = spare[:, 0:TOK * HEADS].rearrange("p (t h) -> p t h", h=HEADS)
        bias_sb = sb("bias_sb", [P, HEADS, TOK])
        gmat = sb("gmat", [P, P])
        ones = sb("ones", [P, P])
        stats = sb("stats", [P, BK, NCHUNK, 6])
        mv = sb("mv", [P, BK, 2])
        rmax = sb("rmax", [P, 2, WP * HEADS])
        rsum = sb("rsum", [P, 2, WP * HEADS])
        rinv = sb("rinv", [P, 2, WP * HEADS])
        gsc = sb("gsc", [P, BK])
        gsh = sb("gsh", [P, BK])
        fin_a = sb("fin_a", [P, BK])
        fin_d = sb("fin_d", [P, BK])
        prm = sb("prm", [P, 4, KC])
        rate = sb("rate", [P, 2])
        sc = sb("sc", [P, 35, 16])
        cube = sb("cube", [P, 2, 64])
        with ExitStack() as pass1:
            def sb1(name, shape):
                return pass1.enter_context(nc.sbuf_tensor(name, shape, f32r))
            xhi_all = sb1("xhi_all", [P, 2, KC, NT])
            xlo_all = sb1("xlo_all", [P, 2, KC, NT])
            ot_all = sb1("ot_all", [P, 2, HP, NT])
            whi = sb1("whi", [P, KC, 4 * CH])
            wlo = sb1("wlo", [P, KC, 4 * CH])
        xhi = [xhi_all[:, i, :, :] for i in range(2)]
        xlo = [xlo_all[:, i, :, :] for i in range(2)]
        ot_hi, ot_lo = ot_all[:, 0, :, :], ot_all[:, 1, :, :]
        late = sb("late", [P, 5, STRIP // KC])

        ps_a0 = pb("ps_a0", [P, 1024])
        ps_a1 = pb("ps_a1", [P, 1024])
        ps_b = pb("ps_b", [P, 1024])
        ps_c = pb("ps_c", [P, 1024])

        w_loaded, par_loaded = sem("w_loaded"), sem("par_loaded")
        relc_done, relrc_done, bias_loaded = sem("relc_done"), sem("relrc_done"), sem("bias_loaded")
        consts_ready, pads_ready = sem("consts_ready"), sem("pads_ready")
        w_hi_ready, w_lo_ready = sem("w_hi_ready"), sem("w_lo_ready")
        pool_chain = sem("pool_chain")
        p0_loaded = [sem(f"p0_loaded{i}") for i in range(SLOTS)]
        p0_stats = sem("p0_stats")
        small = sem("small")
        to_pe, from_pe = sem("to_pe"), sem("from_pe")
        to_act, from_act = sem("to_act"), sem("from_act")
        x_loaded = sem("x_loaded")
        xn0_act, xn0_dve = sem("xn0_act"), sem("xn0_dve")
        xn_ready, xhi_ready, xlo_ready = sem("xn_ready"), sem("xhi_ready"), sem("xlo_ready")
        q_done, k_done, v_done = sem("q_done"), sem("k_done"), sem("v_done")
        s_done, pv_done, out_done = sem("s_done"), sem("pv_done"), sem("out_done")
        q_evac, k_evac, v_evac = sem("q_evac"), sem("k_evac"), sem("v_evac")
        biased, max_ready, shifted, exp_done = sem("biased"), sem("max_ready"), sem("shifted"), sem("exp_done")
        sum_ready, inv_ready, norm_done = sem("sum_ready"), sem("inv_ready"), sem("norm_done")
        pt_ready, o_evac, olo_ready, res_done = sem("pt_ready"), sem("o_evac"), sem("olo_ready"), sem("res_done")
        x1_stats, x1_stored = sem("x1_stats"), sem("x1_stored")
        p2_loaded = [sem(f"p2_loaded{i}") for i in range(SLOTS2)]
        p2_stored = [sem(f"p2_stored{i}") for i in range(SLOTS2)]
        fin_done = sem("fin_done")

        def steps(eng, body, peeled=1):
            def strip(i, first, last):
                for g in range(STEPS_PER_STRIP):
                    body(i, g, lambda lag, g=g: (not first or g >= lag) and (not last or g - lag < STEPS_PER_STRIP))
            for i in range(peeled):
                strip(i, i == 0, False)
            with eng.Fori(peeled, STRIPS - 1) as i:
                strip(i, False, False)
            strip(STRIPS - 1, False, True)
            for g in range(3):
                body(STRIPS, g, lambda lag, g=g: lag > g)

        def slot(eng, i, n):
            return i % n if isinstance(i, int) else eng.snap(i & (n - 1))

        def xs_at(s, k, lo, n):
            v = xs[:, s:s + 1, :] if isinstance(s, int) else xs[:, bass.ds(s, 1), :]
            v = v.rearrange("p a f -> p (a f)")
            return v[:, k * NIMG * ROW + lo:k * NIMG * ROW + lo + n]

        def xn_at(s):
            v = xn[:, s:s + 1, :] if isinstance(s, int) else xn[:, bass.ds(s, 1), :]
            return v.rearrange("p a f -> p (a f)").rearrange("p (k f) -> p k f", k=KC)

        def normalise_aps(eng, i, k, b, w0, w1):
            src = xs_at(slot(eng, i, SLOTS), k, b * ROW, ROW).rearrange("p (r w c) -> p w r c", r=WIN, c=WIN)
            dst = xn_at(slot(eng, i, 2))[:, k, :].rearrange("p (w b r c) -> p b w r c", b=NIMG, r=WIN, c=WIN)[:, b]
            j = b * KC + k
            return dst[:, w0:w1], src[:, w0:w1], gsc[:, j:j + 1], gsh[:, j:j + 1]

        FIRST_PARTS = [(0, WPS), (WPS, STEPS_PER_STRIP * WPS)]

        HALF = STRIP // KC
        p2_bufs = [[xs[:, s, k * HALF:(k + 1) * HALF] for k in range(KC)] for s in range(SLOTS)]
        p2_bufs += [[wf[:].rearrange("p k n -> p (k n)"), spare[:]]]
        p2_bufs += [[xn[:, s, k * HALF:(k + 1) * HALF] for k in range(KC)] for s in range(2)]
        p2_bufs += [[late[:, 0, :], late[:, 1, :]],
                    [v_all[:, 2 * k:2 * k + 2, :, :].rearrange("p i w c -> p (i w c)") for k in range(KC)],
                    [kbd[:].rearrange("p a w h t -> p (a w h t)"), ptbd[:].rearrange("p w a h v t -> p (w a h v t)")],
                    [prob_all[:].rearrange("p i w h t -> p (i w h t)"), late[:, 2, :]],
                    [late[:, 3, :], late[:, 4, :]]]
        assert len(p2_bufs) == SLOTS2
        P2_FIRST = [STRIPS - SLOTS + s for s in range(SLOTS)] + list(range(SLOTS2 - SLOTS))
        P2_FULL, P2_REST = divmod(STRIPS - SLOTS2, SLOTS2)

        def p2_strip(r, s):
            return r * SLOTS2 + (s - SLOTS)

        block = ctx.enter_context(nc.Block())

        @block.sync
        def _(sp):
            def piece(t, q):
                return x_bk[t:t + 1, :, q * STRIP:(q + 1) * STRIP] if isinstance(t, int) else \
                    x_bk[bass.ds(t, 1), :, q * STRIP:(q + 1) * STRIP]
            for q in range(SLOTS):
                sp.dma_start(xs[:, q, :], piece(0, q).rearrange("a p f -> p (a f)")).then_inc(p0_loaded[q], 16)
            with sp.Fori(1, BK) as t:
                read = [sp.snap(t * SLOTS + (q + 1 - SLOTS)) for q in range(SLOTS)]
                for q in range(SLOTS):
                    sp.wait_ge(p0_stats, read[q])
                    sp.dma_start(xs[:, q, :], piece(t, q).rearrange("a p f -> p (a f)")).then_inc(p0_loaded[q], 16)

            sp.dma_start(wf[:, :, 0:3 * CH], w_qkv.rearrange("(k p) n -> p k n", p=P)).then_inc(w_loaded, 16)
            sp.dma_start(wf[:, :, 3 * CH:4 * CH], w_out.rearrange("(k p) n -> p k n", p=P)).then_inc(w_loaded, 16)

            def load(i, s):
                for k in range(KC):
                    src = x_strips[k][i:i + 1] if isinstance(i, int) else x_strips[k][bass.ds(i, 1)]
                    v = xs[:, s:s + 1, :] if isinstance(s, int) else xs[:, bass.ds(s, 1), :]
                    v = v.rearrange("p a f -> p (a f)")[:, k * NIMG * ROW:(k + 1) * NIMG * ROW]
                    sp.dma_start(v.rearrange("p (b f) -> p b f", b=NIMG),
                                 src.rearrange("a p b f -> p (a b) f")).then_inc(x_loaded, 16)

            for i in range(SLOTS - 1):
                sp.wait_ge(p0_stats, (BK - 1) * SLOTS + i + 1)
                if i:
                    sp.wait_ge(x_loaded, 32 * i)
                load(i, i)
            sp.wait_ge(p0_stats, BK * SLOTS)
            sp.wait_ge(x_loaded, 32 * (SLOTS - 1))
            load(SLOTS - 1, SLOTS - 1)

            def store(m, s):
                dst = x1_dram[m:m + 1] if isinstance(m, int) else x1_dram[bass.ds(m, 1)]
                v = xs[:, s:s + 1, :] if isinstance(s, int) else xs[:, bass.ds(s, 1), :]
                sp.dma_start(dst.rearrange("a p f -> p (a f)"), v.rearrange("p a f -> p (a f)")).then_inc(x1_stored, 16)

            with sp.Fori(1, STRIPS - SLOTS + 1) as i:
                s = slot(sp, i + (SLOTS - 1), SLOTS)
                before, ahead = sp.snap(i - 1), sp.snap(i + (SLOTS - 1))
                steps_before, stored, loaded = sp.snap(i * (KC * STEPS_PER_STRIP)), sp.snap(i * 16), sp.snap(i * 32 + 32 * (SLOTS - 1))
                sp.wait_ge(res_done, steps_before)
                store(before, s)
                sp.wait_ge(x1_stats, stored)
                sp.wait_ge(x1_stored, stored)
                sp.wait_ge(x_loaded, loaded)
                load(ahead, s)

            def fetch(m, s):
                for k in range(KC):
                    src = x1_dram[m:m + 1] if isinstance(m, int) else x1_dram[bass.ds(m, 1)]
                    src = src.rearrange("a p f -> p (a f)")[:, k * HALF:(k + 1) * HALF]
                    sp.dma_start(p2_bufs[s][k], src).then_inc(p2_loaded[s], 16)

            free = {SLOTS: [(w_lo_ready, 1)],
                    SLOTS + 1: [(xlo_ready, NSTEP), (xhi_ready, NSTEP)],
                    SLOTS + 3: [(v_done, NSTEP)],
                    SLOTS + 4: [(pv_done, NSTEP)],
                    SLOTS + 6: [(out_done, KC * NSTEP)]}
            sp.wait_ge(x1_stored, 16 * (STRIPS - SLOTS))
            for s in range(SLOTS, SLOTS2):
                for signal, count in free.get(s, []):
                    sp.wait_ge(signal, count)
                fetch(P2_FIRST[s], s)
            with sp.Fori(1, P2_FULL + 1) as r:
                strips = [sp.snap(p2_strip(r, s)) for s in range(SLOTS2)]
                written = sp.snap(r * 32)
                for s in range(SLOTS2):
                    sp.wait_ge(p2_stored[s], written)
                    fetch(strips[s], s)
            for s in range(P2_REST):
                sp.wait_ge(p2_stored[s], 32 * (P2_FULL + 1))
                fetch(p2_strip(P2_FULL + 1, s), s)

        @block.gpsimd
        def _(pool):
            pool.memset(gmat[:], 1.0 / GROUP).then_inc(pool_chain, 1)
            pool.memset(ones[:], 1.0).then_inc(consts_ready, 1)
            pool.wait_ge(pool_chain, 1)
            g3 = gmat[:].rearrange("p (g j) -> p g j", j=GROUP)
            pool.affine_select(out=g3, in_=g3, compare_op=ALU.is_ge, fill=0.0, base=0,
                               pattern=[[-GROUP, P // GROUP], [0, GROUP]], channel_multiplier=1).then_inc(pool_chain, 1)
            pool.wait_ge(pool_chain, 2)
            pool.affine_select(out=g3, in_=g3, compare_op=ALU.is_ge, fill=0.0, base=GROUP - 1,
                               pattern=[[GROUP, P // GROUP], [0, GROUP]], channel_multiplier=-1).then_inc(consts_ready, 1)
            pool.memset(kbd[:], 0.0).then_inc(pads_ready, 1)
            pool.memset(ptbd[:], 0.0).then_inc(pads_ready, 1)
            pool.wait_ge(w_hi_ready, 1)
            pool.tensor_tensor(wlo[:], wf[:], whi[:], ALU.subtract).then_inc(w_lo_ready, 1)

            def low_part(i, g, m):
                src = xn_at(slot(pool, i, 2))[:, :, g * NT:(g + 1) * NT]
                pool.wait_ge(xhi_ready, m + 1)
                pool.tensor_tensor(xlo[g % 2], src, xhi[g % 2], ALU.subtract).then_inc(xlo_ready, 1)

            low_part(0, 0, 0)

            def body(i, g, ok):
                n = i * STEPS_PER_STRIP + g
                if ok(1):
                    pool.wait_ge(max_ready, n)
                    j = (g - 1) % 2
                    p3 = prob[j].rearrange("p w h t -> p (w h) t")
                    pool.tensor_tensor(p3, p3, rmax[:, j, :].unsqueeze(2).broadcast_to([P, WP * HEADS, TOK]),
                                       ALU.subtract).then_inc(shifted, 1)
                if ok(-1):
                    pool_i, pool_g = (i, g + 1) if g + 1 < STEPS_PER_STRIP else (i + 1, 0)
                    low_part(pool_i, pool_g, n + 1)
                if ok(1):
                    pool.wait_ge(inv_ready, n)
                    pool.tensor_tensor(p3, p3, rinv[:, j, :].unsqueeze(2).broadcast_to([P, WP * HEADS, TOK]),
                                       ALU.mult).then_inc(norm_done, 1)

            steps(pool, body)

        @block.scalar
        def _(act):
            for n, v in enumerate((running_mean, running_var, weight, bias)):
                for k in range(KC):
                    act.dma_start(prm[:, n, k:k + 1], v[k * P:(k + 1) * P].unsqueeze(1)).then_inc(par_loaded, 16)
            act.dma_start(rate[:, 0:1], source_rate.broadcast_to([P, 1])).then_inc(par_loaded, 16)

            TE, F = HEADS, PIX * HEADS
            for c1 in range(WIN):
                src = bass.AP(bias_table.tensor, (c1 + WIN - 1) * TE,
                              [[NREL * TE, (2 * MAXN - 1) * NREL], [-TE, WIN], [1, TE]])
                act.dma_start(rel_c[:, c1 * WIN * TE:(c1 + 1) * WIN * TE].rearrange("a (c h) -> a c h", h=TE), src)\
                    .then_inc(relc_done, 16)
            act.wait_ge(relc_done, 16 * WIN)
            for r1 in range(WIN):
                for c1 in range(WIN):
                    src = bass.AP(rel_c.tensor, (r1 + WIN - 1) * F + c1 * WIN * TE,
                                  [[NREL * F, 2 * MAXN - 1], [-F, WIN], [1, WIN * TE]])
                    act.dma_start(rel_rc[:, r1 * WIN + c1, :].rearrange("a (r e) -> a r e", r=WIN), src)\
                        .then_inc(relrc_done, 16)
            act.wait_ge(relrc_done, 16 * PIX)
            for half in range(2):
                for f1 in range(NIMG):
                    src = bass.AP(rel_rc.tensor, (f1 + MAXN - 1) * PIX * F, [[F, PIX], [-PIX * F, NIMG], [1, F]])
                    q0 = half * TOK + f1 * PIX
                    act.dma_start(bias_kh[q0:q0 + PIX].rearrange("p (f t) h -> p f (t h)", f=NIMG), src)\
                        .then_inc(bias_loaded, 16)

            act.wait_ge(w_loaded, 32)
            act.activation(whi[:], wf[:], ACT.Copy).then_inc(w_hi_ready, 1)

            def root(n, src):
                act.wait_ge(to_act, n)
                act.activation(sc[:, 1, 0:src.shape[-1]], src, ACT.Sqrt).then_inc(from_act, 1)

            root(1, sc[:, 0, 0:BK])

            def normalise(i, piece):
                k, b = divmod(piece, NIMG)
                dst, src, scale, shift = normalise_aps(act, i, k, b, 0, STEPS_PER_STRIP * WPS)
                act.activation(dst, src, ACT.Identity, bias=shift, scale=scale).then_inc(xn_ready, 1)

            def high_part(i, g):
                src = xn_at(slot(act, i, 2))[:, :, g * NT:(g + 1) * NT]
                act.activation(xhi[g % 2], src, ACT.Copy).then_inc(xhi_ready, 1)

            act.wait_ge(small, SMALL_GN0)
            act.wait_ge(x_loaded, 32)
            for part, (w0, w1) in enumerate(FIRST_PARTS):
                for b in range(NIMG):
                    dst, src, scale, shift = normalise_aps(act, 0, 0, b, w0, w1)
                    act.activation(dst, src, ACT.Identity, bias=shift, scale=scale).then_inc(xn0_act, 1)
                if part == 0:
                    act.wait_ge(xn0_act, NIMG)
                    act.wait_ge(xn0_dve, NIMG)
                    high_part(0, 0)
            act.wait_ge(pads_ready, 2)

            def body(i, g, ok):
                n = i * STEPS_PER_STRIP + g
                if ok(-STEPS_PER_STRIP):
                    if g == 0:
                        act.wait_ge(x_loaded, i * 32 + 64)
                        if not isinstance(i, int) or i > 0:
                            act.wait_ge(xhi_ready, i * STEPS_PER_STRIP)
                            act.wait_ge(xlo_ready, i * STEPS_PER_STRIP)
                    nxt = i + 1 if isinstance(i, int) else act.snap(i + 1)
                    normalise(nxt, 2 * g)
                    normalise(nxt, 2 * g + 1)
                if ok(-1):
                    if isinstance(i, int) and n == 0:
                        act.wait_ge(xn0_act, 2 * NIMG)
                        act.wait_ge(xn0_dve, 2 * NIMG)
                    if g == STEPS_PER_STRIP - 1:
                        act.wait_ge(xn_ready, i * BK + BK)
                    if ok(1):
                        act.wait_ge(v_done, n)
                        act.wait_ge(xlo_ready, n)
                if ok(0):
                    act.wait_ge(q_done, n + 1)
                    act.activation(q_sb[:].rearrange("p a t -> p (a t)"), ps_a0[:], ACT.Copy, scale=QSCALE).then_inc(q_evac, 1)
                    if ok(-1):
                        if g + 1 < STEPS_PER_STRIP:
                            high_part(i, g + 1)
                        else:
                            high_part(nxt, 0)
                    act.wait_ge(k_done, n + 1)
                    for hh in range(2):
                        rows = slice(hh * DH, (hh + 1) * DH)
                        ins = act.activation(kbd[rows, :, :, hh, :].rearrange("p a w t -> p (a w) t"),
                                             ps_a1[rows, :].rearrange("p (aw t) -> p aw t", t=TOK), ACT.Copy)
                    ins.then_inc(k_evac, 1)
                if ok(1):
                    act.wait_ge(shifted, n)
                    p2 = prob[(g - 1) % 2].rearrange("p w h t -> p (w h t)")
                    act.activation(p2, p2, ACT.Exp).then_inc(exp_done, 1)
                if ok(0):
                    act.wait_ge(v_done, n + 1)
                    act.activation(v_sb[g].rearrange("p w c -> p (w c)"), ps_a0[:], ACT.Copy).then_inc(v_evac, 1)
                if ok(2):
                    act.wait_ge(pv_done, n - 1)
                    act.activation(ot_hi.rearrange("p a t -> p (a t)"), ps_c[:], ACT.Copy).then_inc(o_evac, 1)

            steps(act, body)

            root(2, sc[:, 0, 0:BK])
            root(3, sc[:, 32, 0:NIMG * NIMG:NIMG + 1])
            root(4, sc[:, 0, 0:BK])

            def store(m, s, count):
                act.wait_ge(fin_done, count)
                for k in range(KC):
                    dst = out_strips[k][m:m + 1] if isinstance(m, int) else out_strips[k][bass.ds(m, 1)]
                    act.dma_start(dst.rearrange("a p b f -> p (a b) f"),
                                  p2_bufs[s][k].rearrange("p (b f) -> p b f", b=NIMG))\
                        .then_inc(p2_stored[s], 16)
            for s in range(SLOTS2):
                store(P2_FIRST[s], s, s + 1)
            with act.Fori(1, P2_FULL + 1) as r:
                for s in range(SLOTS2):
                    store(act.snap(p2_strip(r, s)), s, r * SLOTS2 + (s + 1))
            for s in range(P2_REST):
                store(p2_strip(P2_FULL + 1, s), s, (P2_FULL + 1) * SLOTS2 + s + 1)
            for s in range(SLOTS2):
                act.wait_ge(p2_stored[s], 32 * (P2_FULL + 1 + (s < P2_REST)))

        @block.tensor
        def _(pe):
            def small_mm(n, dst, lhsT, parts):
                pe.wait_ge(to_pe, n)
                for j, r in enumerate(parts):
                    ins = pe.matmul(dst, lhsT, r, start=(j == 0), stop=(j == len(parts) - 1))
                ins.then_inc(from_pe, 1)

            pe.wait_ge(consts_ready, 2)

            def group_mms(n):
                small_mm(n, ps_b[:, 0:BK], gmat[:], [mv[:, :, 0]])
                small_mm(n + 1, ps_b[:, 0:BK], gmat[:], [mv[:, :, 1], sc[:, 3, 0:BK]])

            group_mms(1)
            pe.wait_ge(w_hi_ready, 1)
            pe.wait_ge(w_lo_ready, 1)

            def body(i, g, ok):
                n = i * STEPS_PER_STRIP + g
                hi, lo = xhi[g % 2], xlo[g % 2]

                def project_qk(ps, col0):
                    for a in range(HP):
                        cols = slice(col0 + a * P, col0 + (a + 1) * P)
                        terms = [(w[:, k, cols], t[:, k, :]) for k in range(KC) for w, t in ((whi, hi), (whi, lo), (wlo, hi))]
                        for j, (w, t) in enumerate(terms):
                            ins = pe.matmul(ps[:, a * NT:(a + 1) * NT], w, t, start=(j == 0), stop=(j == len(terms) - 1))
                    return ins

                if ok(1):
                    pe.wait_ge(q_evac, n)
                    pe.wait_ge(k_evac, n)
                    if ok(4):
                        pe.wait_ge(res_done, (n - 3) * KC)
                    elif ok(2):
                        pe.wait_ge(biased, n - 1)
                    for w in range(WPS):
                        rows = slice(w % 2 * TOK, (w % 2 + 1) * TOK)
                        for a in range(HP):
                            c = w // 2 * HEADS * TOK + a * 2 * TOK
                            ins = pe.matmul(ps_b[rows, c:c + 2 * TOK], q_sb[:, a, w * TOK:(w + 1) * TOK],
                                            kbd[:, a, w, :, :].rearrange("p h t -> p (h t)"), start=True, stop=True)
                    ins.then_inc(s_done, 1)
                if ok(0):
                    pe.wait_ge(xhi_ready, n + 1)
                    pe.wait_ge(xlo_ready, n + 1)
                    if ok(1):
                        pe.wait_ge(v_evac, n)
                    project_qk(ps_a0, 0).then_inc(q_done, 1)
                    if ok(1):
                        pe.wait_ge(k_evac, n)
                    project_qk(ps_a1, CH).then_inc(k_done, 1)
                if ok(0):
                    pe.wait_ge(q_evac, n + 1)
                    for w in range(WP):
                        toks = slice(w * 2 * TOK, (w + 1) * 2 * TOK)
                        terms = [(t[:, k, toks], wt[:, k, 2 * CH:3 * CH]) for k in range(KC) for t, wt in ((hi, whi), (hi, wlo), (lo, whi))]
                        for j, (t, wt) in enumerate(terms):
                            ins = pe.matmul(ps_a0[:, w * CH:(w + 1) * CH], t, wt, start=(j == 0), stop=(j == len(terms) - 1))
                    ins.then_inc(v_done, 1)
                if ok(3):
                    pe.wait_ge(olo_ready, n - 2)
                    if ok(1):
                        pe.wait_ge(biased, n)
                    else:
                        pe.wait_ge(res_done, (n - 3) * KC)
                    for m in range(KC):
                        terms = [(w[:, k, 3 * CH + m * P:3 * CH + (m + 1) * P], t[:, k, :]) for k in range(KC)
                                 for w, t in ((whi, ot_hi), (whi, ot_lo), (wlo, ot_hi))]
                        for j, (w, t) in enumerate(terms):
                            ins = pe.matmul(ps_b[:, m * NT:(m + 1) * NT], w, t, start=(j == 0), stop=(j == len(terms) - 1))
                        ins.then_inc(out_done, 1)
                if ok(2):
                    pe.wait_ge(pt_ready, n - 1)
                    pe.wait_ge(v_evac, n - 1)
                    for w in range(WP):
                        for a in range(HP):
                            for hh in range(2):
                                h = 2 * a + hh
                                ins = pe.matmul(ps_c[hh * DH:(hh + 1) * DH, a * NT + w * P:a * NT + (w + 1) * P],
                                                v_sb[(g - 2) % 4][:, w, h * DH:(h + 1) * DH],
                                                ptbd[:, w, a, hh, :, :].rearrange("p v t -> p (v t)"), start=True, stop=True)
                    ins.then_inc(pv_done, 1)

            steps(pe, body)
            group_mms(3)
            small_mm(5, ps_b[:, 0:NIMG * NIMG], ones[:], [cube[:, 0, k * 16:(k + 1) * 16] for k in range(KC)])

        @block.vector
        def _(dve):
            chain = [0]

            def link(ins):
                chain[0] += 1
                ins.then_inc(small, 1)
                dve.wait_ge(small, chain[0])

            def aside(ins):
                chain[0] += 1
                ins.then_inc(small, 1)

            asks = {"pe": 0, "act": 0}

            def asked(who):
                asks[who] += 1
                dve.sem_inc(to_pe if who == "pe" else to_act, 1)

            def answered(who):
                dve.wait_ge(from_pe if who == "pe" else from_act, asks[who])

            TT, TS, STT = dve.tensor_tensor, dve.tensor_scalar, dve.scalar_tensor_tensor

            def rsqrt_asked(v):
                asked("act")
                aside(TS(sc[:, 9, 0:v.shape[-1]], v, -0.5, None, ALU.mult))

            def rsqrt(dst):
                n = dst.shape[-1]
                y, minus_half_v, t = sc[:, 1, 0:n], sc[:, 9, 0:n], sc[:, 4, 0:n]
                answered("act")
                link(dve.reciprocal(y, y))
                link(TT(t, y, y, ALU.mult))
                link(TT(t, t, minus_half_v, ALU.mult))
                link(STT(out=dst, in0=t, scalar=1.5, in1=y, op0=ALU.add, op1=ALU.mult))

            def aggregate(rows):
                for j in rows:
                    ins = dve.bn_aggr(mv[:, j, :], stats[:, j, :, :].rearrange("p n s -> p (n s)"))
                return ins

            off = sc[:, 2, 0:BK]

            def group_norm():
                asked("pe")
                answered("pe")
                gm = sc[:, 5, 0:BK]
                aside(dve.tensor_copy(gm, ps_b[:, 0:BK]))
                link(TT(off, mv[:, :, 0], ps_b[:, 0:BK], ALU.subtract))
                link(TT(sc[:, 3, 0:BK], off, off, ALU.mult))
                asked("pe")
                answered("pe")
                link(TS(sc[:, 0, 0:BK], ps_b[:, 0:BK], GN_EPS, None, ALU.add))
                rsqrt_asked(sc[:, 0, 0:BK])
                rsqrt(gsc[:])
                aside(STT(out=gsh[:], in0=gm, scalar=-1.0, in1=gsc[:], op0=ALU.mult, op1=ALU.mult))

            def piece_stats(t, q):
                for j in range(STRIP // 512):
                    c = q * (STRIP // 512) + j
                    dst = stats[:, t:t + 1, c, :] if isinstance(t, int) else stats[:, bass.ds(t, 1), c, :]
                    ins = dve.bn_stats(dst.rearrange("p a s -> p (a s)"), xs[:, q, j * 512:(j + 1) * 512])
                ins.then_inc(p0_stats, 1)
            with dve.Fori(0, BK - 1) as t:
                for q in range(SLOTS):
                    dve.wait_ge(p0_loaded[q], t * 16 + 16)
                    piece_stats(t, q)
            dve.wait_ge(p0_stats, (BK - 1) * SLOTS)
            aggregate(range(BK - 1))
            for q in range(SLOTS):
                dve.wait_ge(p0_loaded[q], BK * 16)
                piece_stats(BK - 1, q)
            dve.wait_ge(p0_stats, BK * SLOTS)
            link(aggregate([BK - 1]))
            group_norm()
            assert chain[0] == SMALL_GN0, chain[0]
            dve.wait_ge(small, SMALL_GN0)
            dve.wait_ge(x_loaded, 32)
            for w0, w1 in FIRST_PARTS:
                for b in range(NIMG):
                    dst, src, scale, shift = normalise_aps(dve, 0, 1, b, w0, w1)
                    TS(dst, src, scale, shift, ALU.mult, ALU.add).then_inc(xn0_dve, 1)
            dve.wait_ge(bias_loaded, 16 * 8)
            link(dve.tensor_copy(bias_sb[:], bias_kh.rearrange("p t h -> p h t")))

            def t(n, w=BK):
                return sc[:, n, 0:w]

            def kb(ap):
                return ap.rearrange("p (b k) -> p k b", k=KC)

            def k3(ap):
                return ap.rearrange("p (k b) -> p k b", k=KC)

            def sq(ap):
                return ap.rearrange("p (i j) -> p i j", j=NIMG)

            def over_i(ap):
                return ap.unsqueeze(2).broadcast_to([P, NIMG, NIMG])

            def over_j(ap):
                return ap.unsqueeze(1).broadcast_to([P, NIMG, NIMG])

            idx, eye, mixed, far = t(14, NIMG), t(15, 16), t(24, 4), t(12, 16)
            for b in range(NIMG):
                link(dve.memset(sc[:, 14, b:b + 1], float(b - NIMG)))
            link(TT(sq(eye), over_i(idx), over_j(idx), ALU.is_equal))
            dve.wait_ge(par_loaded, 16 * (1 + 4 * KC))
            link(TS(rate[:, 0:1], rate[:, 0:1], 0.0, 1.0, ALU.max, ALU.min))
            link(TS(rate[:, 1:2], rate[:, 0:1], -1.0, 1.0, ALU.mult, ALU.add))
            link(TS(mixed, prm[:, 0:2, :].rearrange("p a k -> p (a k)"), rate[:, 0:1], None, ALU.mult))
            link(TS(mixed[:, KC:2 * KC], mixed[:, KC:2 * KC], BN_EPS, None, ALU.add))
            link(TS(far, eye, 1e30, 1.0, ALU.mult, ALU.add))

            def strip_stats(m, pieces):
                s = slot(dve, m, SLOTS)
                for piece in pieces:
                    k, b = divmod(piece, NIMG)
                    dst = stats[:, b * KC + k, m:m + 1, :] if isinstance(m, int) else stats[:, b * KC + k, bass.ds(m, 1), :]
                    ins = dve.bn_stats(dst.rearrange("p a s -> p (a s)"), xs_at(s, k, b * ROW, ROW))
                if piece == BK - 1:
                    ins.then_inc(x1_stats, 16)

            def transpose_probs(pr):
                B = TOK // 2
                for v in range(2):
                    for qh in range(2):
                        for kh in range(2):
                            ins = dve.transpose(
                                ptbd[v * TOK + kh * B:v * TOK + (kh + 1) * B, :, :, :, v, qh * B:(qh + 1) * B]
                                .rearrange("p w a h t -> p (w a h) t"),
                                pr[v * TOK + qh * B:v * TOK + (qh + 1) * B, :, :, kh * B:(kh + 1) * B]
                                .rearrange("p w h t -> p (w h) t"))
                return ins

            dve.wait_ge(pads_ready, 2)

            def body(i, g, ok):
                n = i * STEPS_PER_STRIP + g
                j = (g - 1) % 2
                p3 = prob[j].rearrange("p w h t -> p (w h) t")
                if ok(3):
                    dve.wait_ge(o_evac, n - 2)
                    TT(ot_lo.rearrange("p a t -> p (a t)"), ps_c[:], ot_hi.rearrange("p a t -> p (a t)"),
                       ALU.subtract).then_inc(olo_ready, 1)
                if ok(1):
                    dve.wait_ge(s_done, n)
                    TT(prob[j].rearrange("p w h t -> p w (h t)"), ps_b[:].rearrange("p (w f) -> p w f", w=WP),
                       bias_sb[:].rearrange("p h t -> p (h t)").unsqueeze(1).broadcast_to([P, WP, HEADS * TOK]),
                       ALU.add).then_inc(biased, 1)
                    dve.wait_ge(biased, n)
                    dve.tensor_reduce(rmax[:, j, :], p3, AX.X, ALU.max).then_inc(max_ready, 1)
                if ok(2):
                    dve.wait_ge(norm_done, n - 1)
                    if ok(3):
                        dve.wait_ge(pv_done, n - 2)
                    transpose_probs(prob[g % 2]).then_inc(pt_ready, 1)
                if ok(1):
                    dve.wait_ge(exp_done, n)
                    dve.tensor_reduce(rsum[:, j, :], p3, AX.X, ALU.add).then_inc(sum_ready, 1)
                    dve.wait_ge(sum_ready, n)
                    dve.reciprocal(rinv[:, j, :], rsum[:, j, :]).then_inc(inv_ready, 1)
                last = isinstance(i, int) and i == STRIPS and g == 2
                if ok(3):
                    sg = (g - 3) % 4
                    si = i if g == 3 else (i - 1 if isinstance(i, int) else dve.snap(i - 1))
                    s = slot(dve, si, SLOTS)
                    for m in range(KC):
                        dve.wait_ge(out_done, n * KC - (3 * KC - m - 1))
                        v = xs_at(s, m, 0, NIMG * ROW).rearrange("p (br w) -> p br w", w=W)
                        v = v[:, :, sg * WPS * WIN:(sg + 1) * WPS * WIN].rearrange("p br (j c) -> p br j c", c=WIN)
                        o = ps_b[:, m * NT:(m + 1) * NT].rearrange("p (j br c) -> p br j c", br=NIMG * WIN, c=WIN)
                        ins = TT(v, o, v, ALU.add)
                        ins.then_inc(res_done, 1)
                        if last:
                            dve.wait_ge(res_done, (NSTEP - 1) * KC + m + 1)
                            strip_stats(STRIPS - 1, range(m * NIMG, (m + 1) * NIMG))
                m = (i - 1 if g >= 2 else i - 2) if isinstance(i, int) else dve.snap(i - 1 if g >= 2 else i - 2)
                if not last and (not isinstance(m, int) or m >= 0):
                    if g == 2:
                        dve.wait_ge(res_done, i * (KC * STEPS_PER_STRIP))
                    p = (g - 2) % STEPS_PER_STRIP
                    strip_stats(m, (2 * p, 2 * p + 1))

            steps(dve, body, peeled=2)

            dve.wait_ge(x1_stats, 16 * STRIPS)
            link(aggregate(range(BK)))
            group_norm()

            mu, sg2 = t(7), t(8)
            KII = [P, KC, NIMG, NIMG]
            link(TT(mu, off, gsc[:], ALU.mult))
            g4 = cube[:, 0, 0:KC * NIMG * NIMG].rearrange("p (k i j) -> p k i j", k=KC, i=NIMG)
            link(TT(g4, kb(mu).unsqueeze(3).broadcast_to(KII), kb(mu).unsqueeze(2).broadcast_to(KII), ALU.mult))
            asked("pe")
            gw = t(11)
            wt = prm[:, 2, :].unsqueeze(2).broadcast_to([P, KC, NIMG])
            aside(TS(sg2, mv[:, :, 1], float(HW) / (HW - 1), None, ALU.mult))
            aside(TT(k3(gw), kb(gsc[:]), wt, ALU.mult))
            link(TT(t(10), gsc[:], gsc[:], ALU.mult))
            link(TT(sg2, sg2, t(10), ALU.mult))
            answered("pe")
            gram = t(32, 16)
            link(dve.tensor_copy(gram, ps_b[:, 0:16]))
            rn = t(13, NIMG)
            rsqrt_asked(gram[:, 0:16:NIMG + 1])
            rsqrt(rn)

            dist = t(16, 16)
            link(TT(sq(dist), sq(gram), over_i(rn), ALU.mult))
            link(TT(sq(dist), sq(dist), over_j(rn), ALU.mult))
            link(STT(out=dist, in0=dist, scalar=-1.0, in1=far, op0=ALU.mult, op1=ALU.add))
            dmin, cand, nn = t(17, NIMG), t(18, 16), t(19, NIMG)
            link(dve.tensor_reduce(dmin, sq(dist), AX.X, ALU.min))
            link(TT(sq(cand), sq(dist), over_i(dmin), ALU.is_equal))

            def masked_min(dst, mask, values):
                link(TT(sq(t(21, 16)), sq(mask), over_j(values), ALU.mult))
                link(dve.tensor_reduce(dst, sq(t(21, 16)), AX.X, ALU.min))

            masked_min(nn, cand, idx)
            nbr, adj = t(22, 16), t(23, 16)
            link(TT(sq(nbr), over_i(nn), over_j(idx), ALU.is_equal))
            link(TT(nbr, nbr, eye, ALU.add))
            c3 = cube[:, 0, :].rearrange("p (i j m) -> p i j m", j=NIMG, m=NIMG)
            link(TT(c3, sq(nbr).unsqueeze(2).broadcast_to([P, NIMG, NIMG, NIMG]),
                    sq(nbr).unsqueeze(1).broadcast_to([P, NIMG, NIMG, NIMG]), ALU.mult))
            link(dve.tensor_reduce(sq(adj), c3, AX.X, ALU.add))
            link(TS(adj, adj, 0.0, None, ALU.is_gt))
            lab = [idx] + [t(25 + r, NIMG) for r in range(NIMG - 1)]
            for r in range(NIMG - 1):
                masked_min(lab[r + 1], adj, lab[r])
            part, size = t(28, 16), t(29, NIMG)
            link(TT(sq(part), over_i(lab[-1]), over_j(lab[-1]), ALU.is_equal))
            link(dve.tensor_reduce(size, sq(part), AX.X, ALU.add))
            link(TS(size, size, CL_EPS, None, ALU.add))
            link(dve.reciprocal(size, size))
            link(TT(sq(part), sq(part), over_i(size), ALU.mult))

            c4 = [cube[:, c, 0:32].rearrange("p (k b i) -> p k b i", k=KC, b=NIMG) for c in range(2)]

            def over_cluster(dst, vals):
                link(TT(c4[1], sq(part).unsqueeze(1).broadcast_to(KII), vals, ALU.mult))
                link(dve.tensor_reduce(k3(dst), c4[1], AX.X, ALU.add))

            mug, sgg, v2 = t(33), t(34), sc[:, 0, 0:BK]
            over_cluster(mug, kb(mu).unsqueeze(2).broadcast_to(KII))
            link(TT(c4[0], kb(mu).unsqueeze(2).broadcast_to(KII), k3(mug).unsqueeze(3).broadcast_to(KII), ALU.subtract))
            link(TT(c4[0], c4[0], c4[0], ALU.mult))
            link(TT(c4[0], c4[0], kb(sg2).unsqueeze(2).broadcast_to(KII), ALU.add))
            over_cluster(sgg, c4[0])

            def blend(dst, v, n):
                return STT(out=k3(dst), in0=k3(v), scalar=rate[:, 1:2],
                           in1=mixed[:, n * KC:(n + 1) * KC].unsqueeze(2).broadcast_to([P, KC, NIMG]),
                           op0=ALU.mult, op1=ALU.add)
            link(blend(v2, sgg, 1))
            rsqrt_asked(v2)
            m_all, gm_w, rw = t(31), t(6), t(30)
            link(blend(m_all, mug, 0))
            link(TT(k3(gm_w), kb(gsh[:]), k3(m_all), ALU.subtract))
            link(TT(k3(gm_w), k3(gm_w), wt, ALU.mult))
            rsqrt(rw)
            aside(TT(gw, gw, rw, ALU.mult))
            link(TT(gm_w, gm_w, rw, ALU.mult))
            aside(TS(fin_a[:], gw, 1.0, None, ALU.add))
            link(TT(k3(fin_d[:]), k3(gm_w), prm[:, 3, :].unsqueeze(2).broadcast_to([P, KC, NIMG]), ALU.add))

            def finish(s):
                for k in range(KC):
                    for b in range(NIMG):
                        v, j = p2_bufs[s][k][:, b * ROW:(b + 1) * ROW], k * NIMG + b
                        ins = TS(v, v, fin_a[:, j:j + 1], fin_d[:, j:j + 1], ALU.mult, ALU.add)
                ins.then_inc(fin_done, 1)
            for s in range(SLOTS2):
                if s >= SLOTS:
                    dve.wait_ge(p2_loaded[s], 32)
                finish(s)
            with dve.Fori(1, P2_FULL + 1) as r:
                for s in range(SLOTS2):
                    dve.wait_ge(p2_loaded[s], r * 32 if s < SLOTS else r * 32 + 32)
                    finish(s)
            for s in range(P2_REST):
                dve.wait_ge(p2_loaded[s], 32 * (P2_FULL + 1 + (s >= SLOTS)))
                finish(s)


SMALL_GN0 = 11

_INS = ["x", "L0_conv_w_qkv", "L0_conv_w_out", "L0_conv_bias_table", "L1_conv_running_mean",
        "L1_conv_running_var", "L1_conv_weight", "L1_conv_bias", "L1_conv_source_rate"]
_OUT = ((4, 256, 128, 128), "float32")


def kernel(**inputs):
    import numpy as _np
    import concourse.bacc as _bacc
    from concourse import mybir as _mybir
    from concourse.bass_utils import run_bass_kernel_spmd as _run

    nc = _bacc.Bacc("TRN2", target_bir_lowering=False, num_devices=1)
    arrays, args = {}, []
    for name in _INS:
        a = _np.ascontiguousarray(inputs[name])
        if a.ndim < 1 or name.endswith("source_rate"):
            a = a.reshape(1, 1)
        arrays[f"in_{name}"] = a
        args.append(nc.dram_tensor(f"in_{name}", a.shape, _mybir.dt.from_np(a.dtype), kind="ExternalInput").ap())
    args.append(nc.dram_tensor("out_0", _OUT[0], _mybir.dt.from_np(_np.dtype(_OUT[1])), kind="ExternalOutput").ap())
    conv_preact_kernel(nc, *args)
    r = _run(nc, [arrays], core_ids=[0])
    return r.results[0]["out_0"]
```
